# Optimizing a Trainium2 kernel written in Bass

```python
import numpy as np
import jax
import jax.numpy as jnp

def _softmax(x, axis=-1):
    return jax.nn.softmax(x, axis=axis)

def _gelu(x):
    return jax.nn.gelu(x, approximate=True)

def _silu(x):
    return jax.nn.silu(x)

def _sigmoid(x):
    return jax.nn.sigmoid(x)

def _layernorm(x, axis=-1, eps=1e-05):
    m = jnp.mean(x, axis=axis, keepdims=True)
    v = jnp.var(x, axis=axis, keepdims=True)
    return (x - m) / jnp.sqrt(v + eps)

def _scatter_add(tgt, idx, src, axis=0):
    return tgt.at[idx].add(src)

def _segment_sum(src, seg, n):
    return jax.ops.segment_sum(src, seg, n)
kernel_name = 'mk_xattn_ffn_d1_seqx_r4_b2c291'

def setup_inputs(seed: int=0):
    np.random.seed(seed)
    _w = jnp.asarray

    def _rec_inputs():
        import jax
        import jax.numpy as jnp
        _rk = jax.random.key(seed)
        x = -0.0002928 + 1 * jax.random.normal(jax.random.fold_in(_rk, 1), (32, 128, 256), jnp.float32)
        _lenS = 128 - jax.random.randint(jax.random.fold_in(_rk, 7), (32,), 0, max(1, 128 // 4) + 1, jnp.int32)
        _lenS2 = 128 - jax.random.randint(jax.random.fold_in(_rk, 8), (32,), 0, max(1, 128 // 4) + 1, jnp.int32)
        _ctx_1024P = jax.random.normal(jax.random.fold_in(_rk, 11), (32, 16, 256), jnp.float32)
        _ctx_1024c = jax.random.dirichlet(jax.random.fold_in(_rk, 511), 0.3 * jnp.ones((16,), jnp.float32), (32, 128))
        _ctx_1024t = jnp.einsum('bsk,bkd->bsd', _ctx_1024c, _ctx_1024P)
        _ctx_1024t = _ctx_1024t * jax.lax.rsqrt(jnp.mean(jnp.square(_ctx_1024t)) + 1e-12) * 0.953939
        ctx_1024 = 4.13588e-05 + 0.999923 * (_ctx_1024t + 0.3 * jax.random.normal(jax.random.fold_in(_rk, 611), (32, 128, 256), jnp.float32))
        itok_BxS_8_8191 = jax.random.randint(jax.random.fold_in(_rk, 12), (32, 128), 8, 2048, jnp.int32)
        itok_BxS2_1_8191 = jax.random.randint(jax.random.fold_in(_rk, 13), (32, 128), 1, 2048, jnp.int32)
        _validS = jnp.arange(128)[None, :] < _lenS[:, None]
        _validS2 = jnp.arange(128)[None, :] < _lenS2[:, None]
        _causal = jnp.tril(jnp.ones((128, 128), dtype=bool))
        mask_BxSxS2_if1 = jnp.where(jnp.ones((32, 128, 128), dtype=bool), 1, 0).astype(jnp.int32)
        return (x, ctx_1024, itok_BxS_8_8191, itok_BxS2_1_8191, mask_BxSxS2_if1)
    x, ctx_1024, itok_BxS_8_8191, itok_BxS2_1_8191, mask_BxSxS2_if1 = _rec_inputs()

    def _L0_xattn_setup():
        import jax, jax.numpy as jnp
        import numpy as np
        DIM = 256
        NUM_HEADS = 16
        HEAD_DIM = DIM // NUM_HEADS

        def _slopes(num_heads):
            ratio = 2.0 ** (-8.0 / num_heads)
            return jnp.asarray([ratio ** i for i in range(1, num_heads + 1)], dtype=jnp.float32)
        key = jax.random.key(seed)
        ks = jax.random.split(key, 10)
        b, q_len, k_len = (2, 512, 1024)
        query = jax.random.normal(ks[0], (b, q_len, DIM), dtype=jnp.float32)
        keys = jax.random.normal(ks[1], (b, k_len, DIM), dtype=jnp.float32)
        values = jax.random.normal(ks[2], (b, k_len, DIM), dtype=jnp.float32)
        query_pos = jnp.sort(jax.random.randint(ks[3], (b, q_len), 0, 2048), axis=-1)
        key_pos = jnp.sort(jax.random.randint(ks[4], (b, k_len), 0, 2048), axis=-1)
        mask = jnp.ones((b, q_len, k_len), dtype=jnp.int32)
        lim = float(np.sqrt(6.0 / (DIM + DIM)))
        W_q = jax.random.uniform(ks[5], (DIM, DIM), minval=-lim, maxval=lim, dtype=jnp.float32)
        W_k = jax.random.uniform(ks[6], (DIM, DIM), minval=-lim, maxval=lim, dtype=jnp.float32)
        W_v = jax.random.uniform(ks[7], (DIM, DIM), minval=-lim, maxval=lim, dtype=jnp.float32)
        W_o = jax.random.uniform(ks[8], (DIM, DIM), minval=-lim, maxval=lim, dtype=jnp.float32)
        return {'query': query, 'keys': keys, 'values': values, 'W_q': W_q, 'W_k': W_k, 'W_v': W_v, 'W_o': W_o, 'query_pos': query_pos, 'key_pos': key_pos, 'mask': mask}
    _L0_xattn_all = _L0_xattn_setup()
    _L0_xattn_in = {k: v for k, v in _L0_xattn_all.items() if k in ('W_q', 'W_k', 'W_v', 'W_o')}
    del _L0_xattn_all

    def _L0_ffn_setup():
        import jax, jax.numpy as jnp
        import numpy as np
        D_MODEL = 256
        EXPANSION = 4
        D_HIDDEN = D_MODEL * EXPANSION
        NUM_STAGES = int(np.log2(D_HIDDEN))

        def butterfly(y, weights, dim):
            lead = y.shape[:-1]
            for stage in range(weights.shape[0]):
                s = 2 ** stage
                nb = dim // (2 * s)
                yr = y.reshape(*lead, nb, 2, s)
                a = yr[..., 0, :]
                b = yr[..., 1, :]
                w = weights[stage].reshape(nb, s, 2, 2)
                na = w[..., 0, 0] * a + w[..., 0, 1] * b
                nb2 = w[..., 1, 0] * a + w[..., 1, 1] * b
                y = jnp.stack([na, nb2], axis=-2).reshape(*lead, dim)
            return y
        key = jax.random.key(seed)
        ks = jax.random.split(key, 6)
        B, S = (4, 512)
        x = jax.random.normal(ks[0], (B, S, D_MODEL), jnp.float32)
        W_exp = jax.random.normal(ks[1], (D_MODEL, D_HIDDEN), jnp.float32) * 0.02
        b_exp = jnp.zeros((D_HIDDEN,), jnp.float32)
        up_weights = jax.random.normal(ks[2], (NUM_STAGES, D_HIDDEN // 2, 2, 2), jnp.float32) * 0.02
        up_bias = jnp.zeros((D_HIDDEN,), jnp.float32)
        down_weights = jax.random.normal(ks[3], (NUM_STAGES, D_HIDDEN // 2, 2, 2), jnp.float32) * 0.02
        W_con = jax.random.normal(ks[4], (D_HIDDEN, D_MODEL), jnp.float32) * 0.02
        b_con = jnp.zeros((D_MODEL,), jnp.float32)
        down_bias = jnp.zeros((D_MODEL,), jnp.float32)
        return dict(x=x, W_exp=W_exp, b_exp=b_exp, up_weights=up_weights, up_bias=up_bias, down_weights=down_weights, W_con=W_con, b_con=b_con, down_bias=down_bias)
    _L0_ffn_all = _L0_ffn_setup()
    _L0_ffn_in = {k: v for k, v in _L0_ffn_all.items() if k in ('W_exp', 'b_exp', 'up_weights', 'up_bias', 'down_weights', 'W_con', 'b_con', 'down_bias')}
    del _L0_ffn_all
    return {'x': x, 'ctx_1024': ctx_1024, 'itok_BxS_8_8191': itok_BxS_8_8191, 'itok_BxS2_1_8191': itok_BxS2_1_8191, 'mask_BxSxS2_if1': mask_BxSxS2_if1, 'L0_xattn_W_q': _L0_xattn_in['W_q'], 'L0_xattn_W_k': _L0_xattn_in['W_k'], 'L0_xattn_W_v': _L0_xattn_in['W_v'], 'L0_xattn_W_o': _L0_xattn_in['W_o'], 'L0_ffn_W_exp': _L0_ffn_in['W_exp'], 'L0_ffn_b_exp': _L0_ffn_in['b_exp'], 'L0_ffn_up_weights': _L0_ffn_in['up_weights'], 'L0_ffn_up_bias': _L0_ffn_in['up_bias'], 'L0_ffn_down_weights': _L0_ffn_in['down_weights'], 'L0_ffn_W_con': _L0_ffn_in['W_con'], 'L0_ffn_b_con': _L0_ffn_in['b_con'], 'L0_ffn_down_bias': _L0_ffn_in['down_bias']}

def reference(x, ctx_1024, itok_BxS_8_8191, itok_BxS2_1_8191, mask_BxSxS2_if1, L0_xattn_W_q, L0_xattn_W_k, L0_xattn_W_v, L0_xattn_W_o, L0_ffn_W_exp, L0_ffn_b_exp, L0_ffn_up_weights, L0_ffn_up_bias, L0_ffn_down_weights, L0_ffn_W_con, L0_ffn_b_con, L0_ffn_down_bias):
    import jax
    import jax.numpy as jnp

    def _L0_xattn_ref(query, keys, values, W_q, W_k, W_v, W_o, query_pos, key_pos, mask):
        import jax, jax.numpy as jnp
        import numpy as np
        DIM = 256
        NUM_HEADS = 16
        HEAD_DIM = DIM // NUM_HEADS

        def _slopes(num_heads):
            ratio = 2.0 ** (-8.0 / num_heads)
            return jnp.asarray([ratio ** i for i in range(1, num_heads + 1)], dtype=jnp.float32)
        b, q_len, _ = query.shape
        k_len = keys.shape[1]
        scale = 1.0 / np.sqrt(HEAD_DIM)
        Q = (query @ W_q.T).reshape(b, q_len, NUM_HEADS, HEAD_DIM).transpose(0, 2, 1, 3)
        K = (keys @ W_k.T).reshape(b, k_len, NUM_HEADS, HEAD_DIM).transpose(0, 2, 1, 3)
        V = (values @ W_v.T).reshape(b, k_len, NUM_HEADS, HEAD_DIM).transpose(0, 2, 1, 3)
        scores = jnp.einsum('bhqd,bhkd->bhqk', Q, K) * scale
        dist = (query_pos[:, :, None] - key_pos[:, None, :]).astype(scores.dtype)
        bias = -_slopes(NUM_HEADS)[None, :, None, None] * dist[:, None, :, :]
        scores = scores + bias
        scores = jnp.where(mask[:, None, :, :] == 0, -jnp.inf, scores)
        m = jnp.max(scores, axis=-1, keepdims=True)
        e = jnp.exp(scores - m)
        attn = e / (1.0 + jnp.sum(e, axis=-1, keepdims=True))
        out = jnp.einsum('bhqk,bhkd->bhqd', attn, V)
        out = out.transpose(0, 2, 1, 3).reshape(b, q_len, DIM)
        return out @ W_o.T

    def _L0_ffn_ref(x, W_exp, b_exp, up_weights, up_bias, down_weights, W_con, b_con, down_bias):
        import jax, jax.numpy as jnp
        import numpy as np
        D_MODEL = 256
        EXPANSION = 4
        D_HIDDEN = D_MODEL * EXPANSION
        NUM_STAGES = int(np.log2(D_HIDDEN))

        def butterfly(y, weights, dim):
            lead = y.shape[:-1]
            for stage in range(weights.shape[0]):
                s = 2 ** stage
                nb = dim // (2 * s)
                yr = y.reshape(*lead, nb, 2, s)
                a = yr[..., 0, :]
                b = yr[..., 1, :]
                w = weights[stage].reshape(nb, s, 2, 2)
                na = w[..., 0, 0] * a + w[..., 0, 1] * b
                nb2 = w[..., 1, 0] * a + w[..., 1, 1] * b
                y = jnp.stack([na, nb2], axis=-2).reshape(*lead, dim)
            return y
        h = jnp.einsum('bsd,dh->bsh', x, W_exp) + b_exp
        h = butterfly(h, up_weights, D_HIDDEN)
        h = jax.nn.gelu(h + up_bias, approximate=False)
        h = butterfly(h, down_weights, D_HIDDEN)
        y = jnp.einsum('bsh,hd->bsd', h, W_con) + b_con
        return y + down_bias
    x = x + _L0_xattn_ref(_layernorm(x, axis=-1), ctx_1024, ctx_1024, L0_xattn_W_q, L0_xattn_W_k, L0_xattn_W_v, L0_xattn_W_o, itok_BxS_8_8191, itok_BxS2_1_8191, mask_BxSxS2_if1)
    x = x + _L0_ffn_ref(_layernorm(x, axis=-1), L0_ffn_W_exp, L0_ffn_b_exp, L0_ffn_up_weights, L0_ffn_up_bias, L0_ffn_down_weights, L0_ffn_W_con, L0_ffn_b_con, L0_ffn_down_bias)
    return x

_drawn_inputs = setup_inputs


def setup_inputs(seed=0):
    import zlib

    import numpy as np

    out = dict(_drawn_inputs(seed))
    spreads = {'L0_ffn_b_exp': (0.0, 0.1),
     'L0_ffn_up_bias': (0.0, 0.1),
     'L0_ffn_b_con': (0.0, 0.1),
     'L0_ffn_down_bias': (0.0, 0.1)}
    factors = {}
    for name, (base, spread) in spreads.items():
        noise = np.random.default_rng([zlib.crc32(name.encode()), seed]).standard_normal(out[name].shape)
        drawn = base * np.exp(spread * noise) if base else spread * noise
        out[name] = jnp.asarray(drawn.astype(out[name].dtype))
    for name, factor in factors.items():
        out[name] = (out[name] * factor).astype(out[name].dtype)
    return out
```

```python
from contextlib import ExitStack

import concourse.bass as bass
from concourse import mybir

ALU = mybir.AluOpType
ACT = mybir.ActivationFunctionType
AX_X = mybir.AxisListType.X
F32 = mybir.dt.float32
F32R = mybir.dt.float32r
BF16 = mybir.dt.bfloat16
I32 = mybir.dt.int32

P = 128
BATCHES = 32
DM = 256
KD = DM // P
HEADS, HD = 16, 16
HID = 1024
HC = HID // P
GB = 4
G = BATCHES // GB
GT = GB * P
BLOCK_STAGES = 7
MIX_STAGES = 3
PARTS = 3
HH = 8
VW = 32
EPS = 1e-5
MASKED = -(2.0 ** 100)
SCORE_ROWS = 6 * HD + 2 * PARTS
SCORE_ROWS_M = SCORE_ROWS + PARTS
STACK_DMAS = 11

FACTOR_AT = [HC * (2 ** (k + 1) - 2) for k in range(BLOCK_STAGES)]
FACTOR_N = HC * (2 ** (BLOCK_STAGES + 1) - 2)
MIX_UP = [(k, blk * 2 * s + sub, blk * 2 * s + sub + s, blk * s + sub)
          for k, s in enumerate((1, 2, 4)) for blk in range(HC // (2 * s)) for sub in range(s)]
MIX_DOWN = [x for k in (2, 1, 0) for x in MIX_UP if x[0] == k]


def build(nc, x, ctx_t, masks, pos, slopes, w_attn, w_exp_t, w_con, up_bias, out_bias,
          up_factors, down_factors, up_mix, down_mix, ones, out):
    part_scr = nc.dram_tensor("part_scr", (2, 2, PARTS, DM, GT), BF16).ap()
    pos_scr = nc.dram_tensor("pos_scr", (2, PARTS, P, GT), BF16).ap()
    w2_scr = nc.dram_tensor("w2_scr", (P, HC, DM), F32).ap()
    max_scr = nc.dram_tensor("max_scr", (GB, PARTS * HEADS, P), BF16).ap()

    with ExitStack() as stack:
        def sb(name, shape, dt=F32):
            return stack.enter_context(nc.sbuf_tensor(name, shape, dt))

        def sem(name):
            return stack.enter_context(nc.semaphore(name))

        ident = sb("ident", [P, P])
        ident_bf = sb("ident_bf", [P, P], BF16)
        x_all = sb("x_all", [P, BATCHES, DM])
        w1 = sb("w1", [P, KD, HID])
        hid_bias = sb("hid_bias", [P, HC])
        bias_sum = sb("bias_sum", [P, DM])
        neg_half = sb("neg_half", [P, GB])
        stats = sb("stats", [P, GB, 6])
        mean_var = sb("mean_var", [P, GB, 2])
        var_eps = sb("var_eps", [P, GB])
        rstd = sb("rstd", [P, GB])
        xn = sb("xn", [P, GB, DM])
        xh = sb("xh", [P, KD, GT], F32R)
        xl = sb("xl", [P, KD, GT], F32R)

        psum = stack.enter_context(nc.psum_tensor("psum", [P, 8, 512], F32))

        w_in = sem("w_in")
        waits_passed = sem("waits_passed")
        x_in = [sem(f"x_in{r}") for r in range(2)]
        ctx_in = sem("ctx_in")
        mask_in = sem("mask_in")
        ident_ready = sem("ident_ready")
        ones_ready = sem("ones_ready")
        ones_in = sem("ones_in")
        w_high = sem("w_high")
        w_split = sem("w_split")
        pos_val, pos_hi, pos_rest, pos_mid, pos_split = (sem(f"pos_{n}") for n in ("val", "hi", "rest", "mid", "split"))
        pos_stored = sem("pos_stored")
        grow = sem("grow")
        pre_full = sem("pre_full")
        pre_free = sem("pre_free")
        mix_first = sem("mix_first")
        mix_out = sem("mix_out")
        fin_full = sem("fin_full")
        fin_free = sem("fin_free")
        w2_stored = sem("w2_stored")
        w2_in = sem("w2_in")
        bias_ready = sem("bias_ready")
        stats_done, var_done, eps_done, rstd_done, xn_done = (
            sem(f"{n}_done") for n in ("stats", "var", "eps", "rstd", "xn"))
        bank_full = [sem(f"bank_full{c}") for c in range(2)]
        bank_free = [sem(f"bank_free{c}") for c in range(2)]
        x_high = sem("x_high")
        a_high = sem("a_high")
        ctx_high = sem("ctx_high")
        ctx_split = sem("ctx_split")
        part1_done = sem("part1_done")
        part2_done = sem("part2_done")
        parts_done = sem("parts_done")
        parts_stored = sem("parts_stored")
        mask_ready = sem("mask_ready")
        stack_in = [sem(f"stack_in{r}") for r in range(2)]
        slot_full = [sem(f"slot_full{s}") for s in range(2)]
        slot_free = [sem(f"slot_free{s}") for s in range(2)]
        m_over, m_zero, m_safe, m_hi, m_rest, m_mid, m_split = (
            sem(f"m_{n}") for n in ("over", "zero", "safe", "hi", "rest", "mid", "split"))
        turn_full = sem("turn_full")
        turn_free = sem("turn_free")
        max_stored = [sem(f"max_stored{b}") for b in range(GB)]
        max_in = [sem(f"max_in{b}") for b in range(GB)]
        pv_full = [sem(f"pv_full{s}") for s in range(2)]
        pv_free = sem("pv_free")
        den_done = sem("den_done")
        recip_done = sem("recip_done")
        t_full = [sem(f"t_full{c}") for c in range(2)]
        t_free = [sem(f"t_free{c}") for c in range(2)]
        t_high = sem("t_high")
        h_full = sem("h_full")
        wffn_high = sem("wffn_high")
        wffn_split = sem("wffn_split")
        g_done = sem("g_done")
        g_split = sem("g_split")
        ffn_used = sem("ffn_used")
        res_ready = sem("res_ready")
        y_done = sem("y_done")
        stored = sem("stored")

        def group(p, r):
            return 2 * p + r

        def first(p):
            return isinstance(p, int) and p == 0

        def project_use(p, r):
            return 4 * r if first(p) else 12 * p + 6 * r - 2

        def finish_use(p, r):
            return 46 if isinstance(p, int) and 2 * p + r == G - 1 else 12 * p + 6 * r + 8

        def max_use(p, r):
            return 16 * p + 8 * r

        def exp_use(p, r):
            return 16 * p + 8 * r + 4

        def wait(eng, s, value):
            if not (isinstance(value, int) and value <= 0):
                eng.wait_ge(s, value)

        def wait_apart(eng, s, value):
            if isinstance(value, int):
                wait(eng, s, value)
            else:
                eng.wait_ge(s, value)
                eng.sem_inc(waits_passed, 1)

        def pipeline(eng, norm, finish, project, maxima):
            norm(0, 0); project(0, 0)
            norm(0, 1); project(0, 1); maxima(0, 0)
            with eng.Fori(1, G // 2) as p:
                norm(p, 0); finish(p - 1, 0); project(p, 0); maxima(p - 1, 1)
                norm(p, 1); finish(p - 1, 1); project(p, 1); maxima(p, 0)
            last = G // 2 - 1
            finish(last, 0); maxima(last, 1)
            finish(last, 1)

        def skip(p, r):
            pass

        def norm_measure(dve, g, n):
            xg = x_all[:, bass.ds(GB * g, GB), :]
            for b in range(GB):
                last = nc.vector.bn_stats(stats[:, b, :], xg[:, b, :])
            last.then_inc(stats_done, 1)
            wait_apart(dve, stats_done, n + 1)
            for b in range(GB):
                last = nc.vector.bn_aggr(mean_var[:, b, :], stats[:, b, :])
            last.then_inc(var_done, 1)

        def norm_apply(dve, g, n):
            xg = x_all[:, bass.ds(GB * g, GB), :]
            dve.wait_ge(rstd_done, n + 1)
            for b in range(GB):
                last = nc.vector.tensor_scalar(xn[:, b, :], xg[:, b, :], mean_var[:, b, 0:1], rstd[:, b:b + 1],
                                               ALU.subtract, ALU.mult)
            last.then_inc(xn_done, 1)

        def norm_rstd(pool, n):
            wait_apart(pool, var_done, n + 1)
            nc.gpsimd.tensor_scalar(var_eps[:, :], mean_var[:, :, 1], EPS, None, ALU.add).then_inc(eps_done, 1)
            wait_apart(pool, eps_done, n + 1)
            nc.gpsimd.tensor_tensor(rstd[:, :], var_eps[:, :], neg_half[:, :], ALU.pow).then_inc(rstd_done, 1)

        with ExitStack() as phase:
            def sb1(name, shape, dt=F32):
                return phase.enter_context(nc.sbuf_tensor(name, shape, dt))

            wah = sb1("wah", [P, 4, KD, DM], F32R)
            wal = sb1("wal", [P, 4, KD, DM], F32R)

            with ExitStack() as pre:
                def sb0(name, shape, dt=F32):
                    return pre.enter_context(nc.sbuf_tensor(name, shape, dt))

                wa = sb0("wa", [P, 4, KD, DM])
                wet = sb0("wet", [P, HC, DM + 1])
                wc = sb0("wc", [P, HC, DM])
                upb = sb0("upb", [P, HC])
                outb = sb0("outb", [P, 2, DM])
                factors = [sb0(f"factors{d}", [P, FACTOR_N]) for d in range(2)]
                mixw = [sb0(f"mixw{d}", [P, MIX_STAGES, HC // 2, 4]) for d in range(2)]
                blocks = [[sb0(f"blocks{d}{i}", [P, HC, P]) for i in range(2)] for d in range(2)]
                block_t = sb0("block_t", [P, HC, P])
                up_a = sb0("up_a", [P, HC, DM + 1])
                w2_made = sb0("w2_made", [P, HC, DM])
                down_a = sb0("down_a", [P, HC, DM])
                mix_tmp = sb0("mix_tmp", [P, 4, DM + 1])
                posi = sb0("posi", [P, 2, GT], I32)
                slope = sb0("slope", [P, 2])
                posf = sb0("posf", [P, 2, GT])
                posr = sb0("posr", [P, 2, GT])
                posp = sb0("posp", [P, 2, PARTS, GT], BF16)
                loads = [(wa, w_attn), (slope, slopes), (posi, pos), (factors[0], up_factors),
                         (factors[1], down_factors), (wet, w_exp_t), (wc, w_con), (mixw[0], up_mix),
                         (mixw[1], down_mix), (upb, up_bias), (outb, out_bias)]
                last_block = (BLOCK_STAGES - 1) % 2
                up_bufs = [up_a, wet]
                down_bufs = [wc, down_a]
                up_end, down_end = up_bufs[1], down_bufs[1]
                n_mix = 2 * len(MIX_UP)

                with nc.Block() as block:
                    @block.sync
                    def _(sp):
                        for t, src in loads:
                            sp.dma_start(t[:], src).then_inc(w_in, 16)
                        sp.wait_ge(pos_split, 1)
                        for side in range(2):
                            sp.dma_start(pos_scr[side].rearrange("a p n -> p a n"), posp[:, side]).then_inc(pos_stored, 16)
                        sp.wait_ge(pos_stored, 32)
                        sp.wait_ge(fin_free, 8)
                        sp.dma_start(w2_scr, w2_made[:]).then_inc(w2_stored, 16)
                        sp.wait_ge(w2_stored, 16)

                    @block.gpsimd
                    def _(pool):
                        nc.gpsimd.memset(ident[:, :], 0.0).then_inc(ident_ready, 1)
                        pool.wait_ge(ident_ready, 1)
                        nc.gpsimd.affine_select(out=ident[:, :], in_=ident[:, :], compare_op=ALU.not_equal, fill=1.0,
                                                base=0, pattern=[[-1, P]], channel_multiplier=1).then_inc(ident_ready, 1)
                        pool.wait_ge(ident_ready, 2)
                        nc.gpsimd.tensor_copy(ident_bf[:, :], ident[:, :]).then_inc(ident_ready, 1)
                        nc.gpsimd.memset(neg_half[:, :], -0.5).then_inc(ident_ready, 1)

                    @block.tensor
                    def _(pe):
                        pe.wait_ge(ident_ready, 4)
                        pe.wait_ge(grow, BLOCK_STAGES - 1)
                        pe.wait_ge(w_in, 16 * len(loads))
                        for c in range(HC):
                            if c >= 4:
                                pe.wait_ge(pre_free, c - 3)
                            nc.tensor.matmul(psum[:, c % 4, 0:DM + 1], blocks[0][last_block][:, c, :], wet[:, c, :],
                                             start=True, stop=True).then_inc(pre_full, 1)
                        pe.wait_ge(grow, 2 * (BLOCK_STAGES - 1))
                        for q in range(2):
                            for j in range(4):
                                last = nc.tensor.transpose(psum[:, 4 + q, j * P:(j + 1) * P],
                                                           blocks[1][last_block][:, 4 * q + j, :], ident[:, :])
                            last.then_inc(pre_full, 1)
                        pe.wait_ge(pre_free, HC + 2)
                        pe.wait_ge(mix_out, n_mix * MIX_STAGES // 3)
                        for n in range(4):
                            k, q = n // 2, n % 2
                            for j in range(4):
                                last = nc.tensor.transpose(psum[:, n, j * P:(j + 1) * P],
                                                           up_end[:, 4 * q + j, k * P:(k + 1) * P], ident[:, :])
                            last.then_inc(fin_full, 1)
                        pe.wait_ge(mix_out, 2 * n_mix * MIX_STAGES // 3)
                        for n in range(4):
                            for j in range(2):
                                c = 2 * n + j
                                last = nc.tensor.matmul(psum[:, 4 + n, j * DM:(j + 1) * DM], block_t[:, c, :],
                                                        down_end[:, c, :], start=(j == 0), stop=True,
                                                        skip_group_check=True)
                            last.then_inc(fin_full, 1)

                    def mixes():
                        for d, (bufs, plan) in enumerate(((up_bufs, MIX_UP), (down_bufs, MIX_DOWN))):
                            for n, (k, a, b, pair) in enumerate(plan):
                                step = n // 4
                                src, dst = bufs[step % 2], bufs[1 - step % 2]
                                w = mixw[d][:, k, pair, :]
                                wa0, wb0, wa1, wb1 = (0, 1, 2, 3) if d == 0 else (0, 2, 1, 3)
                                yield d, step, src, dst, a, b, a, w[:, wa0:wa0 + 1], w[:, wb0:wb0 + 1]
                                yield d, step, src, dst, a, b, b, w[:, wa1:wa1 + 1], w[:, wb1:wb1 + 1]

                    @block.scalar
                    def _(act):
                        act.wait_ge(w_in, 16 * len(loads))
                        nc.scalar.activation(wah[:], wa[:], ACT.Copy).then_inc(w_high, 1)
                        for c in range(HC):
                            act.wait_ge(pre_full, c + 1)
                            nc.scalar.activation(up_a[:, c, :], psum[:, c % 4, 0:DM + 1], ACT.Copy).then_inc(pre_free, 1)
                        for q in range(2):
                            act.wait_ge(pre_full, HC + q + 1)
                            nc.scalar.activation(block_t[:, 4 * q:4 * q + 4, :].rearrange("p a b -> p (a b)"),
                                                 psum[:, 4 + q, :], ACT.Copy).then_inc(pre_free, 1)
                        act.wait_ge(pre_free, HC + 2)
                        for n, (d, step, src, dst, a, b, o, wfirst, wsecond) in enumerate(mixes()):
                            if n >= 4:
                                act.wait_ge(mix_out, n - 3)
                            if step and n % 8 == 0:
                                act.wait_ge(mix_out, n)
                            width = src.shape[2]
                            nc.scalar.activation(mix_tmp[:, n % 4, 0:width], src[:, a, :], ACT.Copy,
                                                 scale=wfirst).then_inc(mix_first, 1)
                        for n in range(8):
                            act.wait_ge(fin_full, n + 1)
                            dst = (w1[:, n // 2, (n % 2) * 512:(n % 2 + 1) * 512] if n < 4 else
                                   w2_made[:, 2 * (n - 4):2 * (n - 4) + 2, :].rearrange("p a b -> p (a b)"))
                            nc.scalar.activation(dst, psum[:, n, :], ACT.Copy).then_inc(fin_free, 1)

                    @block.vector
                    def _(dve):
                        dve.wait_ge(w_in, 16 * len(loads))
                        for d in range(2):
                            f = factors[d]
                            for k in range(1, BLOCK_STAGES):
                                n = 2 ** k
                                if k == 1:
                                    prev = f[:, 0:FACTOR_AT[1]].rearrange("p (c j) -> p c j", c=HC)
                                else:
                                    prev = blocks[d][(k - 1) % 2].rearrange("p c j -> p (c j)")[:, 0:HC * n]\
                                        .rearrange("p (c j) -> p c j", c=HC)
                                    dve.wait_ge(grow, d * (BLOCK_STAGES - 1) + k - 1)
                                fac = f[:, FACTOR_AT[k]:FACTOR_AT[k] + 2 * HC * n].rearrange(
                                    "p (c o j) -> p c o j", c=HC, o=2)
                                dst = blocks[d][k % 2].rearrange("p c j -> p (c j)")[:, 0:2 * HC * n].rearrange(
                                    "p (c o j) -> p c o j", c=HC, o=2)
                                nc.vector.tensor_tensor(dst, prev[:, :, None, :].to_broadcast([P, HC, 2, n]), fac,
                                                        ALU.mult).then_inc(grow, 1)
                        dve.wait_ge(w_high, 1)
                        nc.vector.tensor_tensor(wal[:], wa[:], wah[:].bitcast(F32), ALU.subtract).then_inc(w_split, 1)
                        for side in range(2):
                            nc.vector.tensor_scalar(posf[:, side], posi[:, side], slope[:, side:side + 1], None,
                                                    ALU.mult).then_inc(pos_val, 1)
                        dve.wait_ge(pos_val, 2)
                        nc.vector.tensor_copy(posp[:, :, 0], posf[:]).then_inc(pos_hi, 1)
                        dve.wait_ge(pos_hi, 1)
                        nc.vector.tensor_tensor(posr[:], posf[:], posp[:, :, 0], ALU.subtract).then_inc(pos_rest, 1)
                        dve.wait_ge(pos_rest, 1)
                        nc.vector.tensor_copy(posp[:, :, 1], posr[:]).then_inc(pos_mid, 1)
                        dve.wait_ge(pos_mid, 1)
                        nc.vector.tensor_tensor(posp[:, :, 2], posr[:], posp[:, :, 1], ALU.subtract).then_inc(pos_split, 1)
                        nc.vector.tensor_tensor(bias_sum[:], outb[:, 0], outb[:, 1], ALU.add).then_inc(bias_ready, 1)
                        for n, (d, step, src, dst, a, b, o, wfirst, wsecond) in enumerate(mixes()):
                            dve.wait_ge(mix_first, n + 1)
                            if step and n % 8 == 0:
                                dve.wait_ge(mix_out, n)
                            width = src.shape[2]
                            nc.vector.scalar_tensor_tensor(dst[:, o, :], src[:, b, :], wsecond,
                                                           mix_tmp[:, n % 4, 0:width], ALU.mult,
                                                           ALU.add).then_inc(mix_out, 1)
                        dve.wait_ge(mix_out, n_mix)
                        nc.vector.tensor_tensor(hid_bias[:], up_end[:, :, DM], upb[:], ALU.add).then_inc(bias_ready, 1)

            ctx_raw = sb1("ctx_raw", [P, KD, GT])
            mask_raw = sb1("mask_raw", [P, 2, GB, P], I32)
            mask_add = [sb1(f"mask_add{r}", [P, 2, GB, P], BF16) for r in range(2)]
            ch = sb1("ch", [P, KD, GT], F32R)
            cl = sb1("cl", [P, KD, GT], F32R)
            rest = sb1("rest", [P, 2, GT])
            parts = sb1("parts", [P, 4, PARTS, GT], BF16)
            q_stack = [sb1(f"q_stack{r}", [P, HEADS, GT], BF16) for r in range(2)]
            k_stack = [sb1(f"k_stack{r}", [P, HEADS, GT], BF16) for r in range(2)]
            values = [sb1(f"values{r}", [P, GB, HEADS, VW]) for r in range(2)]
            neg_max = sb1("neg_max", [P, GB, HEADS])
            m_tmp = sb1("m_tmp", [P, GB, 4, HEADS])
            m_parts = sb1("m_parts", [P, GB, PARTS, HEADS], BF16)
            max_rows = sb1("max_rows", [PARTS * HEADS, GB, P], BF16)
            exps = [sb1(f"exps{s}", [P, HH, P]) for s in range(2)]
            heads_t = [sb1(f"heads_t{i}", [P, 512]) for i in range(2)]
            den = sb1("den", [P, 2, HEADS])
            recip = sb1("recip", [P, 2, HEADS])
            attn = sb1("attn", [P, GB, DM])

            SLOT = [psum[:, 0:2, :], psum[:, 2:4, :]]
            PV, TURN = psum[:, 4, :], psum[:, 5, :]
            BANK = [psum[:, 6, :], psum[:, 7, :]]

            with nc.Block() as block:
                @block.sync
                def _(sp):
                    def norm(p, r):
                        g = group(p, r)
                        sp.dma_start(x_all[:, bass.ds(GB * g, GB), :],
                                     x[bass.ds(GB * g, GB)].rearrange("b p n -> p b n")).then_inc(x_in[r], 16)
                        wait_apart(sp, ctx_split, g)
                        sp.dma_start(ctx_raw[:], ctx_t[bass.ds(g, 1)].rearrange("g p k n -> p (g k) n"))\
                            .then_inc(ctx_in, 16)
                        wait_apart(sp, mask_ready, g)
                        sp.dma_start(mask_raw[:].rearrange("p s b n -> p (s b) n"),
                                     masks[bass.ds(g, 1)].rearrange("g p s b n -> p (g s b) n"))\
                            .then_inc(mask_in, 16)

                    def project(p, r):
                        g = group(p, r)
                        if not first(p):
                            wait_apart(sp, stack_in[r], 16 * STACK_DMAS * p)
                        for n in range(4):
                            wait_apart(sp, parts_done, 4 * g + n + 1)
                            side, m = n // 2, n % 2
                            sp.dma_start(part_scr[r, side, :, m * P:(m + 1) * P, :].rearrange("a p n -> p a n"),
                                         parts[:, n]).then_inc(parts_stored, 16)
                        wait_apart(sp, parts_stored, 64 * (g + 1))
                        if not first(p):
                            wait_apart(sp, slot_full[1], exp_use(p - 1, r) + GB)
                        for side, st, pieces in ((0, q_stack[r], [(0, 0, 3), (3, 0, 2), (5, 0, 1)]),
                                                 (1, k_stack[r], [(0, 0, 1), (1, 0, 1), (2, 0, 1), (3, 1, 1),
                                                                  (4, 1, 1), (5, 2, 1)])):
                            scr = part_scr[r, side].rearrange("a (i h) n -> (a i) (h n)", h=HEADS)
                            for at, part, n in pieces:
                                sp.dma_start(st[HD * at:HD * (at + n)].rearrange("p h n -> p (h n)"),
                                             scr[HD * part:HD * (part + n)]).then_inc(stack_in[r], 16)
                            row = 6 * HD + (PARTS if side == 0 else 0)
                            sp.dma_start(st[row:row + PARTS],
                                         pos_scr[side][:, bass.ds(HEADS * g, HEADS), :]).then_inc(stack_in[r], 16)

                    def maxima(p, r):
                        g = group(p, r)
                        for b in range(GB + 1):
                            if b < GB:
                                wait_apart(sp, turn_free, max_use(p, r) + b + 1)
                                wait_apart(sp, max_in[b], 16 * g)
                                sp.dma_start(max_scr[b], max_rows[:, b, :]).then_inc(max_stored[b], 16)
                            if b:
                                wait_apart(sp, max_stored[b - 1], 16 * (g + 1))
                                sp.dma_start(q_stack[r][SCORE_ROWS:SCORE_ROWS_M, :, (b - 1) * P:b * P],
                                             max_scr[b - 1].rearrange("(a h) n -> a h n", a=PARTS))\
                                    .then_inc(max_in[b - 1], 16)

                    for r in range(2):
                        for t, a, b in ((q_stack[r], 6 * HD, 6 * HD + PARTS), (k_stack[r], 6 * HD + PARTS, SCORE_ROWS_M)):
                            sp.dma_start(t[a:b].rearrange("p h n -> p (h n)"), ones[0:b - a, :]).then_inc(ones_in, 16)
                    pipeline(sp, norm, skip, project, maxima)
                    for r in range(2):
                        sp.wait_ge(stack_in[r], 16 * STACK_DMAS * G // 2)
                    for b in range(GB):
                        sp.wait_ge(max_in[b], 16 * G)

                @block.gpsimd
                def _(pool):
                    for r in range(2):
                        nc.gpsimd.memset(values[r][:], 1.0).then_inc(ones_ready, 1)

                    def norm(p, r):
                        g = group(p, r)
                        norm_rstd(pool, g)

                    def project(p, r):
                        g = group(p, r)
                        wait_apart(pool, ctx_high, g + 1)
                        nc.gpsimd.tensor_tensor(cl[:], ctx_raw[:], ch[:].bitcast(F32), ALU.subtract)\
                            .then_inc(ctx_split, 1)
                        for n in range(4):
                            wait_apart(pool, part2_done, 4 * g + n + 1)
                            nc.gpsimd.tensor_tensor(parts[:, n, 2], rest[:, n % 2], parts[:, n, 1], ALU.subtract)\
                                .then_inc(parts_done, 1)

                    def maxima(p, r):
                        g = group(p, r)
                        for b in range(GB):
                            n = 4 * g + b + 1
                            nm, t = neg_max[:, b, :], m_tmp[:, b]
                            wait_apart(pool, slot_free[1], max_use(p, r) + b + 1)
                            nc.gpsimd.tensor_scalar(t[:, 0], nm, 2.0 ** 40, None, ALU.mult).then_inc(m_over, 1)
                            wait_apart(pool, m_over, n)
                            nc.gpsimd.tensor_scalar(t[:, 1], t[:, 0], 0.0, None, ALU.mult).then_inc(m_zero, 1)
                            wait_apart(pool, m_zero, n)
                            nc.gpsimd.tensor_tensor(t[:, 2], nm, t[:, 1], ALU.add).then_inc(m_safe, 1)
                            wait_apart(pool, m_safe, n)
                            wait_apart(pool, turn_full, max_use(p, r) + b - 7 if not first(p) else (b + 1 if r else 0))
                            nc.gpsimd.tensor_copy(m_parts[:, b, 0], t[:, 2]).then_inc(m_hi, 1)
                            wait_apart(pool, m_hi, n)
                            nc.gpsimd.tensor_tensor(t[:, 3], t[:, 2], m_parts[:, b, 0], ALU.subtract).then_inc(m_rest, 1)
                            wait_apart(pool, m_rest, n)
                            nc.gpsimd.tensor_copy(m_parts[:, b, 1], t[:, 3]).then_inc(m_mid, 1)
                            wait_apart(pool, m_mid, n)
                            nc.gpsimd.tensor_tensor(m_parts[:, b, 2], t[:, 3], m_parts[:, b, 1], ALU.subtract)\
                                .then_inc(m_split, 1)

                    pipeline(pool, norm, skip, project, maxima)

                @block.scalar
                def _(act):
                    def norm(p, r):
                        g = group(p, r)
                        act.wait_ge(ctx_in, 16 * (g + 1))
                        if first(p):
                            wait(act, bank_full[1], 4 * r)
                        else:
                            act.wait_ge(bank_full[1], 12 * p + 6 * r - 4)
                        nc.scalar.activation(ch[:], ctx_raw[:], ACT.Copy).then_inc(ctx_high, 1)

                    def finish(p, r):
                        g = group(p, r)

                        def exp(b, s):
                            act.wait_ge(slot_full[s], exp_use(p, r) + b + 1)
                            if b:
                                act.wait_ge(pv_full[s], 4 * g + b)
                            nc.scalar.activation(exps[s][:].rearrange("p h n -> p (h n)"),
                                                 SLOT[s].rearrange("p a n -> p (a n)"), ACT.Exp).then_inc(slot_free[s], 1)

                        def take_heads(b):
                            act.wait_ge(pv_full[1], 4 * g + b + 1)
                            if b >= 2:
                                act.wait_ge(turn_full, exp_use(p, r) + b - 1)
                            nc.scalar.activation(heads_t[b % 2][:], PV, ACT.Copy).then_inc(pv_free, 1)

                        for b in range(GB):
                            exp(b, 0)
                            exp(b, 1)
                            if b:
                                take_heads(b - 1)
                        take_heads(GB - 1)
                        for c in range(2):
                            act.wait_ge(bank_full[c], finish_use(p, r) + 1)
                            nc.scalar.activation(xh[:, c, :], BANK[c], ACT.Copy).then_inc(a_high, 1)

                    def project(p, r):
                        g = group(p, r)
                        u = project_use(p, r)
                        for c in range(2):
                            act.wait_ge(bank_full[c], u + 1)
                            nc.scalar.activation(xh[:, c, :], BANK[c], ACT.Copy).then_inc(x_high, 1)
                        wait(act, parts_stored, 64 * g)

                        def second_part(n):
                            act.wait_ge(bank_free[n % 2], u + 2 + n // 2)
                            nc.scalar.activation(parts[:, n, 1], rest[:, n % 2], ACT.Copy).then_inc(part2_done, 1)

                        for n in range(4):
                            act.wait_ge(bank_full[n % 2], u + 2 + n // 2)
                            nc.scalar.activation(parts[:, n, 0], BANK[n % 2], ACT.Copy,
                                                 scale=HD ** -0.5 if n < 2 else 1.0).then_inc(part1_done, 1)
                            if n:
                                second_part(n - 1)
                        second_part(3)
                        if first(p):
                            act.wait_ge(ones_ready, 2)
                        for c in range(2):
                            act.wait_ge(bank_full[c], u + 4)
                            nc.scalar.activation(values[r][:, 2 * c:2 * c + 2, :, 0:HD],
                                                 BANK[c].rearrange("p (b h d) -> p b h d", b=2, h=HEADS),
                                                 ACT.Copy).then_inc(bank_free[c], 1)

                    def maxima(p, r):
                        g = group(p, r)
                        for b in range(GB):
                            act.wait_ge(turn_full, max_use(p, r) + b + 1)
                            wait(act, max_stored[b], 16 * g)
                            nc.scalar.activation(max_rows[:, b, :], TURN.bitcast(BF16)[0:PARTS * HEADS, 0:P],
                                                 ACT.Copy).then_inc(turn_free, 1)

                    pipeline(act, norm, finish, project, maxima)

                @block.vector
                def _(dve):
                    dve.wait_ge(fin_free, 8)

                    def norm(p, r):
                        g = group(p, r)
                        dve.wait_ge(x_in[r], 16 * (p + 1))
                        norm_measure(dve, g, g)
                        norm_apply(dve, g, g)

                    def finish(p, r):
                        g = group(p, r)
                        u = finish_use(p, r)
                        turned = TURN.rearrange("p (h v) -> p h v", v=VW)
                        for b in range(GB):
                            n = 4 * g + b + 1
                            dve.wait_ge(turn_full, exp_use(p, r) + b + 1)
                            nc.vector.tensor_scalar(den[:, b % 2], turned[:, :, HD], 1.0, None, ALU.add)\
                                .then_inc(den_done, 1)
                            dve.wait_ge(den_done, n)
                            nc.vector.reciprocal(recip[:, b % 2], den[:, b % 2]).then_inc(recip_done, 1)
                            dve.wait_ge(recip_done, n)
                            nc.vector.tensor_tensor(attn[:, b].rearrange("p (h d) -> p h d", d=HD), turned[:, :, 0:HD],
                                                    recip[:, b % 2][:, :, None].to_broadcast([P, HEADS, HD]),
                                                    ALU.mult).then_inc(turn_free, 1)
                        for c in range(2):
                            dve.wait_ge(a_high, 2 * g + c + 1)
                            nc.vector.tensor_tensor(xl[:, c, :], BANK[c], xh[:, c, :].bitcast(F32), ALU.subtract)\
                                .then_inc(bank_free[c], 1)
                        for c in range(2):
                            dve.wait_ge(bank_full[c], u + 2)
                            xg = x_all[:, bass.ds(GB * g + 2 * c, 2), :].rearrange("p b n -> p (b n)")
                            nc.vector.tensor_tensor(xg, BANK[c], xg, ALU.add).then_inc(bank_free[c], 1)

                    def project(p, r):
                        g = group(p, r)
                        u = project_use(p, r)
                        for c in range(2):
                            dve.wait_ge(x_high, 2 * g + c + 1)
                            nc.vector.tensor_tensor(xl[:, c, :], BANK[c], xh[:, c, :].bitcast(F32), ALU.subtract)\
                                .then_inc(bank_free[c], 1)
                        dve.wait_ge(mask_in, 16 * (g + 1))
                        if not first(p):
                            dve.wait_ge(slot_full[1], exp_use(p - 1, r) + GB)
                        nc.vector.tensor_scalar(mask_add[r][:], mask_raw[:], 0.0, MASKED, ALU.is_equal, ALU.mult)\
                            .then_inc(mask_ready, 1)
                        for n in range(4):
                            dve.wait_ge(part1_done, 4 * g + n + 1)
                            wait(dve, parts_done, 4 * g + n - 1)
                            nc.vector.scalar_tensor_tensor(rest[:, n % 2], BANK[n % 2], HD ** -0.5 if n < 2 else 1.0,
                                                           parts[:, n, 0], ALU.mult, ALU.subtract)\
                                .then_inc(bank_free[n % 2], 1)

                    def maxima(p, r):
                        g = group(p, r)
                        for b in range(GB):
                            wait(dve, m_split, 4 * g + b - 3)
                            for s in range(2):
                                dve.wait_ge(slot_full[s], max_use(p, r) + b + 1)
                                nc.vector.tensor_reduce(neg_max[:, b, s * HH:(s + 1) * HH],
                                                        SLOT[s].rearrange("p a (h n) -> p (a h) n", n=P),
                                                        AX_X, ALU.max, negate=True).then_inc(slot_free[s], 1)

                    pipeline(dve, norm, finish, project, maxima)

                @block.tensor
                def _(pe):
                    pe.wait_ge(fin_free, 8)
                    pe.wait_ge(w_split, 1)

                    def score_half(s, use, b, r, rows, transposed):
                        wait(pe, slot_free[s], use)
                        keep, move = (k_stack[r], q_stack[r]) if transposed else (q_stack[r], k_stack[r])
                        tok = slice(b * P, (b + 1) * P)
                        for q in range(2):
                            dst = SLOT[s][:, q, :]
                            nc.tensor.matmul(dst.rearrange("p (h n) -> p h n", n=P), ident_bf[:, :],
                                             mask_add[r][:, int(transposed), b:b + 1, :].to_broadcast([P, 4, P]),
                                             start=True, stop=False, skip_group_check=True)
                            for j in range(4):
                                h = s * HH + 4 * q + j
                                last = nc.tensor.matmul(dst[:, j * P:(j + 1) * P], keep[0:rows, h, tok],
                                                        move[0:rows, h, tok], start=False, stop=(j == 3),
                                                        skip_group_check=True)
                        last.then_inc(slot_full[s], 1)

                    def split_product(dst, pairs, first_in_bank):
                        terms = [(l, r_) for (lh, ll), (rh, rl) in pairs for l, r_ in ((lh, rh), (ll, rh), (lh, rl))]
                        for i, (l, r_) in enumerate(terms):
                            last = nc.tensor.matmul(dst, l, r_, start=(first_in_bank and i == 0),
                                                    stop=(i == len(terms) - 1), skip_group_check=True)
                        return last

                    def tokens_product(use, xa, xb_, w):
                        for c in range(2):
                            wait(pe, bank_free[c], use)
                            for j in range(2):
                                tok = slice((2 * c + j) * P, (2 * c + j + 1) * P)
                                last = split_product(BANK[c][:, j * DM:(j + 1) * DM],
                                                     [((xa[:, k, tok], xb_[:, k, tok]), (wah[:, w, k, :], wal[:, w, k, :]))
                                                      for k in range(KD)], j == 0)
                            last.then_inc(bank_full[c], 1)

                    def project(p, r):
                        g = group(p, r)
                        u = project_use(p, r)
                        pe.wait_ge(xn_done, g + 1)
                        for c in range(2):
                            wait(pe, bank_free[c], u)
                            for b in range(GB):
                                last = nc.tensor.transpose(BANK[c][:, b * P:(b + 1) * P], xn[:, b, c * P:(c + 1) * P],
                                                           ident[:, :])
                            last.then_inc(bank_full[c], 1)
                        for w, (a_h, a_l) in enumerate(((xh, xl), (ch, cl))):
                            if w == 0:
                                for c in range(2):
                                    pe.wait_ge(bank_free[c], u + 1)
                            else:
                                pe.wait_ge(ctx_split, g + 1)
                            for m in range(2):
                                wait(pe, bank_free[m], u + 1 + w)
                                cols = slice(m * P, (m + 1) * P)
                                split_product(BANK[m],
                                              [((wah[:, w, k, cols], wal[:, w, k, cols]), (a_h[:, k, :], a_l[:, k, :]))
                                               for k in range(KD)], True).then_inc(bank_full[m], 1)
                        tokens_product(u + 3, ch, cl, 2)

                    def turn_max(p, r, b):
                        pe.wait_ge(m_split, 4 * group(p, r) + b + 1)
                        wait_apart(pe, turn_free, max_use(p, r) + b)
                        nc.tensor.transpose(TURN.bitcast(BF16)[0:PARTS * HEADS, 0:P],
                                            m_parts[:, b].rearrange("p a h -> p (a h)"), ident_bf[:, :])\
                            .then_inc(turn_full, 1)

                    def maxima(p, r):
                        pe.wait_ge(ones_in, 64)
                        pe.wait_ge(stack_in[r], 16 * STACK_DMAS * (p + 1))
                        pe.wait_ge(mask_ready, group(p, r) + 1)
                        for b in range(GB):
                            for s in range(2):
                                score_half(s, max_use(p, r) + b, b, r, SCORE_ROWS, False)
                            if b:
                                turn_max(p, r, b - 1)
                        turn_max(p, r, GB - 1)

                    def finish(p, r):
                        g = group(p, r)
                        u = finish_use(p, r)

                        def weigh(b, s):
                            pe.wait_ge(slot_free[s], exp_use(p, r) + b + 1)
                            if s == 0 and b:
                                pe.wait_ge(pv_free, 4 * g + b)
                            for i in range(HH):
                                h = s * HH + i
                                j = i % 4
                                last = nc.tensor.matmul(PV[VW * j:VW * (j + 1), (h // 4) * P:(h // 4 + 1) * P],
                                                        values[r][:, b, h, :], exps[s][:, i, :], start=True, stop=True)
                            last.then_inc(pv_full[s], 1)

                        def turn_heads(b):
                            pe.wait_ge(pv_free, 4 * g + b + 1)
                            wait(pe, turn_free, exp_use(p, r) + b)
                            for q in range(4):
                                last = nc.tensor.transpose(TURN[:, q * P:(q + 1) * P],
                                                           heads_t[b % 2][:, q * P:(q + 1) * P], ident[:, :])
                            last.then_inc(turn_full, 1)

                        def turn_attn(b):
                            pe.wait_ge(turn_free, exp_use(p, r) + b + 1)
                            for c in range(2):
                                if b == 0:
                                    wait(pe, bank_free[c], u)
                                last = nc.tensor.transpose(BANK[c][:, b * P:(b + 1) * P],
                                                           attn[:, b, c * P:(c + 1) * P], ident[:, :])
                                if b == GB - 1:
                                    last.then_inc(bank_full[c], 1)

                        for b in range(GB + 2):
                            for s in range(2):
                                if b < GB:
                                    if s == 0:
                                        pe.wait_ge(max_in[b], 16 * (g + 1))
                                    score_half(s, exp_use(p, r) + b, b, r, SCORE_ROWS_M, True)
                                if 1 <= b <= GB:
                                    weigh(b - 1, s)
                            if 1 <= b <= GB:
                                turn_heads(b - 1)
                            if b >= 2:
                                turn_attn(b - 2)
                        for c in range(2):
                            pe.wait_ge(bank_free[c], u + 1)
                        tokens_product(u + 1, xh, xl, 3)

                    pipeline(pe, skip, finish, project, maxima)

        w2 = sb("w2", [P, HC, DM])
        w1h = sb("w1h", [P, KD, HID], F32R)
        w1l = sb("w1l", [P, KD, HID], F32R)
        w2h = sb("w2h", [P, HC, DM], F32R)
        w2l = sb("w2l", [P, HC, DM], F32R)
        gh = sb("gh", [P, 2, GT], F32R)
        gl = sb("gl", [P, 2, GT], F32R)
        gf = sb("gf", [P, 2, GT])
        x_res = sb("x_res", [P, GB, DM])
        y_out = sb("y_out", [P, GB, DM])
        T = [psum[:, c, :] for c in range(2)]
        HB = [psum[:, 2 + i, :] for i in range(2)]
        Y = [psum[:, 4 + c, :] for c in range(2)]

        def weight_pieces():
            for q in range(4):
                yield tuple(t[:, :, q * DM:(q + 1) * DM] for t in (w1, w1h, w1l))
                yield tuple(t[:, 2 * q:2 * q + 2, :] for t in (w2, w2h, w2l))

        with nc.Block() as block:
            @block.sync
            def _(sp):
                sp.dma_start(w2[:], w2_scr).then_inc(w2_in, 16)
                with sp.Fori(0, G) as g:
                    wait_apart(sp, y_done, 2 * g + 2)
                    sp.dma_start(out[bass.ds(GB * g, GB)].rearrange("b p n -> p b n"), y_out[:]).then_inc(stored, 16)
                sp.wait_ge(stored, 16 * G)

            @block.gpsimd
            def _(pool):
                def residual(g):
                    wait_apart(pool, stored, 16 * g)
                    nc.gpsimd.tensor_tensor(x_res[:], x_all[:, bass.ds(GB * g, GB), :],
                                            bias_sum[:, None, :].to_broadcast([P, GB, DM]), ALU.add)\
                        .then_inc(res_ready, 1)

                norm_rstd(pool, G)
                residual(0)
                with pool.Fori(1, G) as g:
                    norm_rstd(pool, g + G)
                    residual(g)

            @block.scalar
            def _(act):
                def take_tokens(g):
                    for c in range(2):
                        act.wait_ge(t_full[c], g + 1)
                        nc.scalar.activation(xh[:, c, :], T[c], ACT.Copy).then_inc(t_high, 1)

                def hidden(g):
                    for c in range(HC):
                        act.wait_ge(h_full, 8 * g + c + 1)
                        if c >= 2:
                            act.wait_ge(ffn_used, 8 * g + c - 1)
                        nc.scalar.activation(gf[:, c % 2], HB[c % 2], ACT.Gelu, bias=hid_bias[:, c:c + 1])
                        nc.scalar.activation(gh[:, c % 2], HB[c % 2], ACT.Gelu, bias=hid_bias[:, c:c + 1])\
                            .then_inc(g_done, 1)

                take_tokens(0)
                for n, (whole, high, low) in enumerate(weight_pieces()):
                    if n == 1:
                        act.wait_ge(w2_in, 16)
                    nc.scalar.activation(high, whole, ACT.Copy).then_inc(wffn_high, 1)
                with act.Fori(0, G - 1) as g:
                    hidden(g)
                    take_tokens(g + 1)
                hidden(G - 1)

            @block.vector
            def _(dve):
                def split_tokens(g):
                    for c in range(2):
                        dve.wait_ge(t_high, 2 * g + c + 1)
                        nc.vector.tensor_tensor(xl[:, c, :], T[c], xh[:, c, :].bitcast(F32), ALU.subtract)\
                            .then_inc(t_free[c], 1)

                def hidden(g, chunks):
                    for c in chunks:
                        dve.wait_ge(g_done, 8 * g + c + 1)
                        nc.vector.tensor_tensor(gl[:, c % 2], gf[:, c % 2], gh[:, c % 2].bitcast(F32), ALU.subtract)\
                            .then_inc(g_split, 1)

                def finish(g):
                    dve.wait_ge(res_ready, g + 1)
                    dve.wait_ge(ffn_used, 8 * g + 8)
                    for c in range(2):
                        nc.vector.tensor_tensor(y_out[:, 2 * c:2 * c + 2].rearrange("p b n -> p (b n)"), Y[c],
                                                x_res[:, 2 * c:2 * c + 2].rearrange("p b n -> p (b n)"), ALU.add)\
                            .then_inc(y_done, 1)

                norm_measure(dve, 0, G)
                norm_apply(dve, 0, G)
                split_tokens(0)
                for n, (whole, high, low) in enumerate(weight_pieces()):
                    if n == 1:
                        dve.wait_ge(w2_in, 16)
                    dve.wait_ge(wffn_high, n + 1)
                    nc.vector.tensor_tensor(low, whole, high.bitcast(F32), ALU.subtract).then_inc(wffn_split, 1)
                with dve.Fori(0, G - 1) as g:
                    hidden(g, range(2))
                    norm_measure(dve, g + 1, g + 1 + G)
                    hidden(g, range(2, 5))
                    norm_apply(dve, g + 1, g + 1 + G)
                    hidden(g, range(5, HC))
                    split_tokens(g + 1)
                    finish(g)
                hidden(G - 1, range(HC))
                finish(G - 1)

            @block.tensor
            def _(pe):
                def turn_tokens(g):
                    pe.wait_ge(xn_done, g + 1 + G)
                    for c in range(2):
                        wait(pe, t_free[c], g)
                        for b in range(GB):
                            last = nc.tensor.transpose(T[c][:, b * P:(b + 1) * P], xn[:, b, c * P:(c + 1) * P],
                                                       ident[:, :])
                        last.then_inc(t_full[c], 1)

                def up(g, c):
                    pe.wait_ge(wffn_split, 2 * (c // 2) + 1)
                    if c >= 2:
                        pe.wait_ge(g_done, 8 * g + c - 1)
                    n = 0
                    cols = slice(c * P, (c + 1) * P)
                    for k in range(KD):
                        for w, t in ((w1h, xh), (w1l, xh), (w1h, xl)):
                            last = nc.tensor.matmul(HB[c % 2], w[:, k, cols], t[:, k, :], start=(n == 0),
                                                    stop=(n == 5))
                            n += 1
                    last.then_inc(h_full, 1)

                def down(g, c):
                    pe.wait_ge(g_split, 8 * g + c + 1)
                    pe.wait_ge(wffn_split, 2 * (c // 2) + 2)
                    for b in range(GB):
                        tok = slice(b * P, (b + 1) * P)
                        for i, (t, w) in enumerate(((gh, w2h), (gl, w2h), (gh, w2l))):
                            last = nc.tensor.matmul(Y[b // 2][:, (b % 2) * DM:(b % 2 + 1) * DM], t[:, c % 2, tok],
                                                    w[:, c, :], start=(c == 0 and i == 0 and b % 2 == 0),
                                                    stop=(c == HC - 1 and i == 2), skip_group_check=True)
                    last.then_inc(ffn_used, 1)

                def group_ffn(g, ahead):
                    for c in range(2):
                        pe.wait_ge(t_free[c], g + 1)
                    for c in range(HC):
                        up(g, c)
                        if c:
                            down(g, c - 1)
                    if ahead:
                        turn_tokens(g + 1)
                    down(g, HC - 1)

                turn_tokens(0)
                with pe.Fori(0, G - 1) as g:
                    group_ffn(g, True)
                group_ffn(G - 1, False)


def _mix_weights(w, np):
    out = np.empty((P, MIX_STAGES, HC // 2, 4), w.dtype)
    for k, _, _, pair in MIX_UP:
        out[:, k, pair] = w[BLOCK_STAGES + k, pair * P:(pair + 1) * P].reshape(P, 4)
    return out


def _block_factors(w, np):
    i = np.arange(P)[:, None, None, None]
    c = np.arange(HC)[None, :, None, None]
    out = []
    for k in range(BLOCK_STAGES):
        o = np.arange(2)[None, None, :, None]
        low = np.arange(2 ** k)[None, None, None, :]
        pair = (c * P + i >> (k + 1)) * 2 ** k + low
        out.append(w[k][pair, o, (i >> k) & 1].reshape(P, -1))
    return np.concatenate(out, 1)


def kernel(x, ctx_1024, itok_BxS_8_8191, itok_BxS2_1_8191, mask_BxSxS2_if1, L0_xattn_W_q, L0_xattn_W_k,
           L0_xattn_W_v, L0_xattn_W_o, L0_ffn_W_exp, L0_ffn_b_exp, L0_ffn_up_weights, L0_ffn_up_bias,
           L0_ffn_down_weights, L0_ffn_W_con, L0_ffn_b_con, L0_ffn_down_bias):
    import numpy as np
    import concourse.bacc as bacc
    from concourse.bass_utils import run_bass_kernel_spmd

    def arr(a):
        return np.asarray(a)

    mask = arr(mask_BxSxS2_if1).reshape(G, GB, P, P)
    pos = np.stack([arr(itok_BxS_8_8191), arr(itok_BxS2_1_8191)], 0).reshape(2, G, 1, GT)
    ratio = 2.0 ** (-8.0 / HEADS)
    slope = np.array([ratio ** i for i in range(1, HEADS + 1)], np.float32)

    def by_chunk(a):
        return a.reshape(-1, P, a.shape[-1]).transpose(1, 0, 2)

    def side_order(w):
        return w.T.reshape(DM, HEADS, HD).transpose(0, 2, 1).reshape(DM, DM)

    weights = [side_order(arr(L0_xattn_W_q)), side_order(arr(L0_xattn_W_k)), arr(L0_xattn_W_v).T, arr(L0_xattn_W_o).T]
    arrays = {
        "x": arr(x),
        "ctx_t": arr(ctx_1024).reshape(G, GT, KD, P).transpose(0, 3, 2, 1),
        "masks": np.stack([mask.transpose(0, 2, 1, 3), mask.transpose(0, 3, 1, 2)], 2),
        "pos": np.broadcast_to(pos, (2, G, HEADS, GT)).reshape(2, P, GT).transpose(1, 0, 2),
        "slopes": np.tile(np.stack([-slope, slope], 1), (G, 1)),
        "w_attn": np.stack([by_chunk(w) for w in weights], 1),
        "w_exp_t": by_chunk(np.concatenate([arr(L0_ffn_W_exp).T, arr(L0_ffn_b_exp)[:, None]], 1)),
        "w_con": by_chunk(arr(L0_ffn_W_con)),
        "up_bias": arr(L0_ffn_up_bias).reshape(HC, P).T,
        "out_bias": np.broadcast_to(np.stack([arr(L0_ffn_b_con), arr(L0_ffn_down_bias)]), (P, 2, DM)),
        "up_factors": _block_factors(arr(L0_ffn_up_weights), np),
        "down_factors": _block_factors(arr(L0_ffn_down_weights), np),
        "up_mix": _mix_weights(arr(L0_ffn_up_weights), np),
        "down_mix": _mix_weights(arr(L0_ffn_down_weights), np),
        "ones": np.ones((2 * PARTS, HEADS * GT), mybir.dt.np(BF16)),
    }
    arrays = {n: np.ascontiguousarray(a) for n, a in arrays.items()}
    nc = bacc.Bacc("TRN2", target_bir_lowering=False, num_devices=1)
    args = [nc.dram_tensor(f"in_{n}", a.shape, mybir.dt.from_np(a.dtype), kind="ExternalInput").ap()
            for n, a in arrays.items()]
    args.append(nc.dram_tensor("out_x", (BATCHES, P, DM), F32, kind="ExternalOutput").ap())
    build(nc, *args)
    r = run_bass_kernel_spmd(nc, [{f"in_{n}": a for n, a in arrays.items()}], core_ids=[0])
    return r.results[0]["out_x"]
```

```python
from collections import namedtuple
from contextlib import ExitStack

import concourse.bass as bass
from concourse import mybir

ALU = mybir.AluOpType
ACT = mybir.ActivationFunctionType
AX_X = mybir.AxisListType.X
F32 = mybir.dt.float32
F32R = mybir.dt.float32r
BF16 = mybir.dt.bfloat16
I32 = mybir.dt.int32

P = 128
BATCHES = 32
DM = 256
KD = DM // P
HEADS, HD = 16, 16
HID = 1024
HC = HID // P
GB = 4
G = BATCHES // GB
GT = GB * P
BLOCK_STAGES = 7
MIX_STAGES = 3
PARTS = 3
HH = 8
VW = 32
EPS = 1e-5
MASKED = -(2.0 ** 100)
SCORE_ROWS = 6 * HD + 2 * PARTS
SCORE_ROWS_M = SCORE_ROWS + PARTS
STACK_DMAS = 11

FACTOR_AT = [HC * (2 ** (k + 1) - 2) for k in range(BLOCK_STAGES)]
FACTOR_N = HC * (2 ** (BLOCK_STAGES + 1) - 2)
MIX_UP = [(k, blk * 2 * s + sub, blk * 2 * s + sub + s, blk * s + sub)
          for k, s in enumerate((1, 2, 4)) for blk in range(HC // (2 * s)) for sub in range(s)]
MIX_DOWN = [x for k in (2, 1, 0) for x in MIX_UP if x[0] == k]


def build(nc, x, ctx_t, masks, pos, slopes, w_attn, w_exp_t, w_con, up_bias, out_bias,
          up_factors, down_factors, up_mix, down_mix, ones, out):
    part_scr = nc.dram_tensor("part_scr", (2, 2, PARTS, DM, GT), BF16).ap()
    pos_scr = nc.dram_tensor("pos_scr", (2, PARTS, P, GT), BF16).ap()
    w1_scr = nc.dram_tensor("w1_scr", (P, KD, HID), F32).ap()
    w2_scr = nc.dram_tensor("w2_scr", (P, HC, DM), F32).ap()
    max_scr = nc.dram_tensor("max_scr", (GB, PARTS * HEADS, P), BF16).ap()

    with ExitStack() as stack:
        def sb(name, shape, dt=F32):
            return stack.enter_context(nc.sbuf_tensor(name, shape, dt))

        def sem(name):
            return stack.enter_context(nc.semaphore(name))

        ident = sb("ident", [P, P])
        ident_bf = sb("ident_bf", [P, P], BF16)
        x_all = sb("x_all", [P, BATCHES, DM])
        hid_bias = sb("hid_bias", [P, HC])
        bias_sum = sb("bias_sum", [P, DM])
        neg_half = sb("neg_half", [P, GB])
        stats = sb("stats", [P, GB, 6])
        mean_var = sb("mean_var", [P, GB, 2])
        var_eps = sb("var_eps", [P, GB])
        rstd = sb("rstd", [P, GB])
        xn = sb("xn", [P, GB, DM])
        xh = sb("xh", [P, KD, GT], F32R)
        xl = sb("xl", [P, KD, GT], F32R)

        psum = stack.enter_context(nc.psum_tensor("psum", [P, 8, 512], F32))

        w_in = sem("w_in")
        waits_passed = sem("waits_passed")
        x_in = [sem(f"x_in{r}") for r in range(2)]
        ctx_in = sem("ctx_in")
        mask_in = sem("mask_in")
        ident_ready = sem("ident_ready")
        ones_ready = sem("ones_ready")
        ones_in = sem("ones_in")
        w_high = sem("w_high")
        w_split = sem("w_split")
        pos_val, pos_hi, pos_rest, pos_mid, pos_split = (sem(f"pos_{n}") for n in ("val", "hi", "rest", "mid", "split"))
        pos_stored = sem("pos_stored")
        grow = sem("grow")
        pre_full = sem("pre_full")
        pre_free = sem("pre_free")
        mix_first = sem("mix_first")
        mix_out = sem("mix_out")
        fin_full = sem("fin_full")
        fin_free = sem("fin_free")
        w_stored = sem("w_stored")
        w1_in = sem("w1_in")
        w2_in = sem("w2_in")
        bias_ready = sem("bias_ready")
        stats_done, var_done, eps_done, rstd_done, xn_done = (
            sem(f"{n}_done") for n in ("stats", "var", "eps", "rstd", "xn"))
        slot_full = [sem(f"slot_full{s}") for s in range(2)]
        half_full = [sem(f"half_full{s}") for s in range(2)]
        slot_free = [sem(f"slot_free{s}") for s in range(2)]
        pair_full = [sem(f"pair_full{c}") for c in range(2)]
        pair_free = [sem(f"pair_free{c}") for c in range(2)]
        turn_full = sem("turn_full")
        turn_free = sem("turn_free")
        pv_full = sem("pv_full")
        pv_free = sem("pv_free")
        x_high, a_high, ctx_high, ctx_split = (
            sem(n) for n in ("x_high", "a_high", "ctx_high", "ctx_split"))
        part1_done, rest_done, part2_done, parts_done, parts_stored = (
            sem(n) for n in ("part1_done", "rest_done", "part2_done", "parts_done", "parts_stored"))
        mask_ready = sem("mask_ready")
        stack_in = [[sem(f"stack_in{r}{half}") for half in range(2)] for r in range(2)]
        m_over, m_zero, m_safe, m_hi, m_rest, m_mid, m_split = (
            sem(n) for n in ("m_over", "m_zero", "m_safe", "m_hi", "m_rest", "m_mid", "m_split"))
        max_stored = [sem(f"max_stored{b}") for b in range(GB)]
        max_in = [sem(f"max_in{b}") for b in range(GB)]
        den_done = sem("den_done")
        recip_done = sem("recip_done")
        t_full = [sem(f"t_full{c}") for c in range(2)]
        t_free = [sem(f"t_free{c}") for c in range(2)]
        t_high = sem("t_high")
        h_full = sem("h_full")
        wffn_high = sem("wffn_high")
        wffn_split = sem("wffn_split")
        g_done = sem("g_done")
        g_split = sem("g_split")
        ffn_used = sem("ffn_used")
        res_ready = sem("res_ready")
        y_done = sem("y_done")
        stored = sem("stored")

        Group = namedtuple("Group", "n start turn")
        FIRST_STEP, LOOP_STEP, LOOP_TURNS, LAST_STEP = -2, 1, 2, G

        def stages(step):
            return [g if 0 <= g < G else None for g in (step, step - 1, step + 2, step + 1)]

        SCORE_T = [("exp", 1, 2 * GB), ("turn_x", 2, 1), ("query", 2, 1)]
        SCORE = [("max", 0, 2 * GB), ("value", 3, 1), ("output", 1, 1)]
        PAIR = [("attn", 1, 1), ("key", 2, 1)]

        def counts(uses):
            table, done = {}, 0
            for step in range(FIRST_STEP, LAST_STEP + 1):
                for name, stage, number in uses:
                    g = stages(step)[stage]
                    if g is not None:
                        table[name, g] = done
                        done += number
            return table

        slot_table = [counts(SCORE_T), counts(SCORE)]
        pair_table = counts(PAIR)
        half_table = [counts(t[1:]) for t in (SCORE_T, SCORE)]
        turn_table, turned = {}, 0
        for step in range(FIRST_STEP, LAST_STEP + 1):
            here = [(n, g) for n, g in zip(("rows", "heads"), stages(step)) if g is not None]
            for n, g in here:
                turn_table[n, g] = (turned + (len(here) == 2 and n == "rows"), len(here))
            turned += GB * len(here)

        def at(table, name, g):
            value = table[name, g.start]
            if isinstance(g.turn, int) and g.turn == 0 and isinstance(g.n, int):
                return value
            by = table[name, g.start + 2] - value
            return value + by * g.turn

        def turn_at(name, g, b):
            first, by = turn_table[name, g.start]
            if isinstance(g.n, int):
                return first + by * b
            return first + by * b + 2 * GB * 2 * g.turn

        def wait(eng, s, value):
            if not (isinstance(value, int) and value <= 0):
                eng.wait_ge(s, value)

        def wait_apart(eng, s, value):
            if isinstance(value, int):
                wait(eng, s, value)
            else:
                eng.wait_ge(s, value)
                eng.sem_inc(waits_passed, 1)

        def pipeline(eng, step):
            def groups(first, turn=0):
                return [None if g is None else Group(g + 2 * turn, g, turn) for g in stages(first)]

            for j in range(FIRST_STEP, LOOP_STEP):
                step(*groups(j))
            with eng.Fori(0, LOOP_TURNS) as turn:
                step(*groups(LOOP_STEP, turn))
                step(*groups(LOOP_STEP + 1, turn))
            for j in range(LOOP_STEP + 2 * LOOP_TURNS, LAST_STEP + 1):
                step(*groups(j))

        def norm_measure(dve, g, n):
            xg = x_all[:, bass.ds(GB * g, GB), :]
            for b in range(GB):
                last = nc.vector.bn_stats(stats[:, b, :], xg[:, b, :])
            last.then_inc(stats_done, 1)
            wait_apart(dve, stats_done, n + 1)
            for b in range(GB):
                last = nc.vector.bn_aggr(mean_var[:, b, :], stats[:, b, :])
            last.then_inc(var_done, 1)

        def norm_apply(dve, g, n):
            xg = x_all[:, bass.ds(GB * g, GB), :]
            dve.wait_ge(rstd_done, n + 1)
            for b in range(GB):
                last = nc.vector.tensor_scalar(xn[:, b, :], xg[:, b, :], mean_var[:, b, 0:1], rstd[:, b:b + 1],
                                               ALU.subtract, ALU.mult)
            last.then_inc(xn_done, 1)

        def norm_rstd(pool, n):
            wait_apart(pool, var_done, n + 1)
            nc.gpsimd.tensor_scalar(var_eps[:, :], mean_var[:, :, 1], EPS, None, ALU.add).then_inc(eps_done, 1)
            wait_apart(pool, eps_done, n + 1)
            nc.gpsimd.tensor_tensor(rstd[:, :], var_eps[:, :], neg_half[:, :], ALU.pow).then_inc(rstd_done, 1)

        with ExitStack() as phase:
            def sb1(name, shape, dt=F32):
                return phase.enter_context(nc.sbuf_tensor(name, shape, dt))

            wah = sb1("wah", [P, 4, KD, DM], F32R)
            wal = sb1("wal", [P, 4, KD, DM], F32R)

            with ExitStack() as pre:
                def sb0(name, shape, dt=F32):
                    return pre.enter_context(nc.sbuf_tensor(name, shape, dt))

                wa = sb0("wa", [P, 4, KD, DM])
                wet = sb0("wet", [P, HC, DM + 1])
                wc = sb0("wc", [P, HC, DM])
                upb = sb0("upb", [P, HC])
                outb = sb0("outb", [P, 2, DM])
                factors = [sb0(f"factors{d}", [P, FACTOR_N]) for d in range(2)]
                mixw = [sb0(f"mixw{d}", [P, MIX_STAGES, HC // 2, 4]) for d in range(2)]
                blocks = [[sb0(f"blocks{d}{i}", [P, HC, P]) for i in range(2)] for d in range(2)]
                block_t = sb0("block_t", [P, HC, P])
                up_a = sb0("up_a", [P, HC, DM + 1])
                w1_made = sb0("w1_made", [P, KD, HID])
                w2_made = sb0("w2_made", [P, HC, DM])
                down_a = sb0("down_a", [P, HC, DM])
                mix_tmp = sb0("mix_tmp", [P, 4, DM + 1])
                posi = sb0("posi", [P, 2, GT], I32)
                slope = sb0("slope", [P, 2])
                posf = sb0("posf", [P, 2, GT])
                posr = sb0("posr", [P, 2, GT])
                posp = sb0("posp", [P, 2, PARTS, GT], BF16)
                loads = [(wa, w_attn), (slope, slopes), (posi, pos), (factors[0], up_factors),
                         (factors[1], down_factors), (wet, w_exp_t), (wc, w_con), (mixw[0], up_mix),
                         (mixw[1], down_mix), (upb, up_bias), (outb, out_bias)]
                last_block = (BLOCK_STAGES - 1) % 2
                up_bufs = [up_a, wet]
                down_bufs = [wc, down_a]
                up_end, down_end = up_bufs[1], down_bufs[1]
                n_mix = 2 * len(MIX_UP)

                with nc.Block() as block:
                    @block.sync
                    def _(sp):
                        for t, src in loads:
                            sp.dma_start(t[:], src).then_inc(w_in, 16)
                        sp.wait_ge(pos_split, 1)
                        for side in range(2):
                            sp.dma_start(pos_scr[side].rearrange("a p n -> p a n"), posp[:, side]).then_inc(pos_stored, 16)
                        sp.wait_ge(pos_stored, 32)
                        sp.wait_ge(fin_free, 8)
                        sp.dma_start(w1_scr, w1_made[:]).then_inc(w_stored, 16)
                        sp.dma_start(w2_scr, w2_made[:]).then_inc(w_stored, 16)
                        sp.wait_ge(w_stored, 32)

                    @block.gpsimd
                    def _(pool):
                        nc.gpsimd.memset(ident[:, :], 0.0).then_inc(ident_ready, 1)
                        pool.wait_ge(ident_ready, 1)
                        nc.gpsimd.affine_select(out=ident[:, :], in_=ident[:, :], compare_op=ALU.not_equal, fill=1.0,
                                                base=0, pattern=[[-1, P]], channel_multiplier=1).then_inc(ident_ready, 1)
                        pool.wait_ge(ident_ready, 2)
                        nc.gpsimd.tensor_copy(ident_bf[:, :], ident[:, :]).then_inc(ident_ready, 1)
                        nc.gpsimd.memset(neg_half[:, :], -0.5).then_inc(ident_ready, 1)

                    @block.tensor
                    def _(pe):
                        pe.wait_ge(ident_ready, 4)
                        pe.wait_ge(grow, BLOCK_STAGES - 1)
                        pe.wait_ge(w_in, 16 * len(loads))
                        for c in range(HC):
                            if c >= 4:
                                pe.wait_ge(pre_free, c - 3)
                            nc.tensor.matmul(psum[:, c % 4, 0:DM + 1], blocks[0][last_block][:, c, :], wet[:, c, :],
                                             start=True, stop=True).then_inc(pre_full, 1)
                        pe.wait_ge(grow, 2 * (BLOCK_STAGES - 1))
                        for q in range(2):
                            for j in range(4):
                                last = nc.tensor.transpose(psum[:, 4 + q, j * P:(j + 1) * P],
                                                           blocks[1][last_block][:, 4 * q + j, :], ident[:, :])
                            last.then_inc(pre_full, 1)
                        pe.wait_ge(pre_free, HC + 2)
                        pe.wait_ge(mix_out, n_mix * MIX_STAGES // 3)
                        for n in range(4):
                            k, q = n // 2, n % 2
                            for j in range(4):
                                last = nc.tensor.transpose(psum[:, n, j * P:(j + 1) * P],
                                                           up_end[:, 4 * q + j, k * P:(k + 1) * P], ident[:, :])
                            last.then_inc(fin_full, 1)
                        pe.wait_ge(mix_out, 2 * n_mix * MIX_STAGES // 3)
                        for n in range(4):
                            for j in range(2):
                                c = 2 * n + j
                                last = nc.tensor.matmul(psum[:, 4 + n, j * DM:(j + 1) * DM], block_t[:, c, :],
                                                        down_end[:, c, :], start=(j == 0), stop=True,
                                                        skip_group_check=True)
                            last.then_inc(fin_full, 1)

                    def mixes():
                        for d, (bufs, plan) in enumerate(((up_bufs, MIX_UP), (down_bufs, MIX_DOWN))):
                            for n, (k, a, b, pair) in enumerate(plan):
                                step = n // 4
                                src, dst = bufs[step % 2], bufs[1 - step % 2]
                                w = mixw[d][:, k, pair, :]
                                wa0, wb0, wa1, wb1 = (0, 1, 2, 3) if d == 0 else (0, 2, 1, 3)
                                yield d, step, src, dst, a, b, a, w[:, wa0:wa0 + 1], w[:, wb0:wb0 + 1]
                                yield d, step, src, dst, a, b, b, w[:, wa1:wa1 + 1], w[:, wb1:wb1 + 1]

                    @block.scalar
                    def _(act):
                        act.wait_ge(w_in, 16 * len(loads))
                        nc.scalar.activation(wah[:], wa[:], ACT.Copy).then_inc(w_high, 1)
                        for c in range(HC):
                            act.wait_ge(pre_full, c + 1)
                            nc.scalar.activation(up_a[:, c, :], psum[:, c % 4, 0:DM + 1], ACT.Copy).then_inc(pre_free, 1)
                        for q in range(2):
                            act.wait_ge(pre_full, HC + q + 1)
                            nc.scalar.activation(block_t[:, 4 * q:4 * q + 4, :].rearrange("p a b -> p (a b)"),
                                                 psum[:, 4 + q, :], ACT.Copy).then_inc(pre_free, 1)
                        act.wait_ge(pre_free, HC + 2)
                        for n, (d, step, src, dst, a, b, o, wfirst, wsecond) in enumerate(mixes()):
                            if n >= 4:
                                act.wait_ge(mix_out, n - 3)
                            if step and n % 8 == 0:
                                act.wait_ge(mix_out, n)
                            width = src.shape[2]
                            nc.scalar.activation(mix_tmp[:, n % 4, 0:width], src[:, a, :], ACT.Copy,
                                                 scale=wfirst).then_inc(mix_first, 1)
                        for n in range(8):
                            act.wait_ge(fin_full, n + 1)
                            dst = (w1_made[:, n // 2, (n % 2) * 512:(n % 2 + 1) * 512] if n < 4 else
                                   w2_made[:, 2 * (n - 4):2 * (n - 4) + 2, :].rearrange("p a b -> p (a b)"))
                            nc.scalar.activation(dst, psum[:, n, :], ACT.Copy).then_inc(fin_free, 1)

                    @block.vector
                    def _(dve):
                        dve.wait_ge(w_in, 16 * len(loads))
                        for d in range(2):
                            f = factors[d]
                            for k in range(1, BLOCK_STAGES):
                                n = 2 ** k
                                if k == 1:
                                    prev = f[:, 0:FACTOR_AT[1]].rearrange("p (c j) -> p c j", c=HC)
                                else:
                                    prev = blocks[d][(k - 1) % 2].rearrange("p c j -> p (c j)")[:, 0:HC * n]\
                                        .rearrange("p (c j) -> p c j", c=HC)
                                    dve.wait_ge(grow, d * (BLOCK_STAGES - 1) + k - 1)
                                fac = f[:, FACTOR_AT[k]:FACTOR_AT[k] + 2 * HC * n].rearrange(
                                    "p (c o j) -> p c o j", c=HC, o=2)
                                dst = blocks[d][k % 2].rearrange("p c j -> p (c j)")[:, 0:2 * HC * n].rearrange(
                                    "p (c o j) -> p c o j", c=HC, o=2)
                                nc.vector.tensor_tensor(dst, prev[:, :, None, :].to_broadcast([P, HC, 2, n]), fac,
                                                        ALU.mult).then_inc(grow, 1)
                        dve.wait_ge(w_high, 1)
                        nc.vector.tensor_tensor(wal[:], wa[:], wah[:].bitcast(F32), ALU.subtract).then_inc(w_split, 1)
                        for side in range(2):
                            nc.vector.tensor_scalar(posf[:, side], posi[:, side], slope[:, side:side + 1], None,
                                                    ALU.mult).then_inc(pos_val, 1)
                        dve.wait_ge(pos_val, 2)
                        nc.vector.tensor_copy(posp[:, :, 0], posf[:]).then_inc(pos_hi, 1)
                        dve.wait_ge(pos_hi, 1)
                        nc.vector.tensor_tensor(posr[:], posf[:], posp[:, :, 0], ALU.subtract).then_inc(pos_rest, 1)
                        dve.wait_ge(pos_rest, 1)
                        nc.vector.tensor_copy(posp[:, :, 1], posr[:]).then_inc(pos_mid, 1)
                        dve.wait_ge(pos_mid, 1)
                        nc.vector.tensor_tensor(posp[:, :, 2], posr[:], posp[:, :, 1], ALU.subtract).then_inc(pos_split, 1)
                        nc.vector.tensor_tensor(bias_sum[:], outb[:, 0], outb[:, 1], ALU.add).then_inc(bias_ready, 1)
                        for n, (d, step, src, dst, a, b, o, wfirst, wsecond) in enumerate(mixes()):
                            dve.wait_ge(mix_first, n + 1)
                            if step and n % 8 == 0:
                                dve.wait_ge(mix_out, n)
                            width = src.shape[2]
                            nc.vector.scalar_tensor_tensor(dst[:, o, :], src[:, b, :], wsecond,
                                                           mix_tmp[:, n % 4, 0:width], ALU.mult,
                                                           ALU.add).then_inc(mix_out, 1)
                        dve.wait_ge(mix_out, n_mix)
                        nc.vector.tensor_tensor(hid_bias[:], up_end[:, :, DM], upb[:], ALU.add).then_inc(bias_ready, 1)

            ctx_raw = sb1("ctx_raw", [P, KD, GT])
            mask_raw = sb1("mask_raw", [P, 2, GB, P], I32)
            mask_add = [sb1(f"mask_add{r}", [P, 2, GB, P], BF16) for r in range(2)]
            ch = sb1("ch", [P, KD, GT], F32R)
            cl = sb1("cl", [P, KD, GT], F32R)
            rest = sb1("rest", [P, 2, GT])
            parts = sb1("parts", [P, 4, PARTS, GT], BF16)
            q_stack = [sb1(f"q_stack{r}", [P, HEADS, GT], BF16) for r in range(2)]
            k_stack = [sb1(f"k_stack{r}", [P, HEADS, GT], BF16) for r in range(2)]
            values = [sb1(f"values{r}", [P, GB, HEADS, VW]) for r in range(2)]
            neg_max = sb1("neg_max", [P, GB, HEADS])
            m_tmp = sb1("m_tmp", [P, GB, 4, HEADS])
            m_parts = sb1("m_parts", [P, GB, PARTS, HEADS], BF16)
            max_rows = sb1("max_rows", [PARTS * HEADS, GB, P], BF16)
            exps = [sb1(f"exps{s}", [P, HH, P]) for s in range(2)]
            ah = sb1("ah", [P, KD, GT], F32R)
            al = sb1("al", [P, KD, GT], F32R)
            heads_t = [sb1(f"heads_t{i}", [P, 512]) for i in range(2)]
            den = sb1("den", [P, 2, HEADS])
            recip = sb1("recip", [P, 2, HEADS])
            attn = sb1("attn", [P, GB, DM])

            SLOT = [psum[:, 0:2, :], psum[:, 2:4, :]]
            PV, TURN = psum[:, 4, :], psum[:, 5, :]
            PAIR_BANK = [psum[:, 6, :], psum[:, 7, :]]
            HALF_TOKENS = [slice(0, GT // 2), slice(GT // 2, GT)]

            def use(s, name, g):
                return at(slot_table[s], name, g)

            def bank_is_full(eng, s, name, g, c):
                if c == 0:
                    eng.wait_ge(half_full[s], at(half_table[s], name, g) + 1)
                else:
                    eng.wait_ge(slot_full[s], use(s, name, g) + 1)

            def round_of(g):
                return g.start // 2 + g.turn

            with nc.Block() as block:
                @block.sync
                def _(sp):
                    def load_x(g, n_round):
                        sp.dma_start(x_all[:, bass.ds(GB * g, GB), :],
                                     x[bass.ds(GB * g, GB)].rearrange("b p n -> p b n")).then_inc(x_in[n_round], 16)

                    def load_ctx(g):
                        sp.dma_start(ctx_raw[:], ctx_t[bass.ds(g, 1)].rearrange("g p k n -> p (g k) n"))\
                            .then_inc(ctx_in, 16)

                    def max_rows_in(g, b):
                        wait_apart(sp, turn_free, turn_at("rows", g, b) + 1)
                        wait_apart(sp, max_in[b], 16 * g.n)
                        sp.dma_start(max_scr[b], max_rows[:, b, :]).then_inc(max_stored[b], 16)
                        wait_apart(sp, max_stored[b], 16 * (g.n + 1))
                        sp.dma_start(q_stack[g.start % 2][SCORE_ROWS:SCORE_ROWS_M, :, b * P:(b + 1) * P],
                                     max_scr[b].rearrange("(a h) n -> a h n", a=PARTS)).then_inc(max_in[b], 16)

                    def load_stacks(g, attend, half):
                        r = g.start % 2
                        if half == 0:
                            wait_apart(sp, parts_stored, 64 * (g.n + 1))
                        if attend is not None:
                            wait_apart(sp, slot_full[0], use(0, "exp", attend) + GB * (half + 1))
                        tok = HALF_TOKENS[half]
                        for side, st, pieces in ((0, q_stack[r], [(0, 0, 3), (3, 0, 2), (5, 0, 1)]),
                                                 (1, k_stack[r], [(0, 0, 1), (1, 0, 1), (2, 0, 1), (3, 1, 1),
                                                                  (4, 1, 1), (5, 2, 1)])):
                            scr = part_scr[r, side].rearrange("a (i h) n -> (a i) h n", h=HEADS)
                            for row, part, n in pieces:
                                sp.dma_start(st[HD * row:HD * (row + n), :, tok],
                                             scr[HD * part:HD * (part + n), :, tok]).then_inc(stack_in[r][half], 16)
                            row = 6 * HD + (PARTS if side == 0 else 0)
                            sp.dma_start(st[row:row + PARTS, :, tok], pos_scr[side][:, bass.ds(HEADS * g.n, HEADS), tok])\
                                .then_inc(stack_in[r][half], 16)

                    def step(maxima, attend, project, value):
                        if project and project.start + 1 < G:
                            load_x(project.n + 1, (project.start + 1) % 2)
                        for b in range(GB):
                            if maxima:
                                max_rows_in(maxima, b)
                            if value and b in (0, 2):
                                load_stacks(value, attend, b // 2)
                        if project:
                            g = project
                            wait_apart(sp, mask_ready, g.n)
                            sp.dma_start(mask_raw[:].rearrange("p s b n -> p (s b) n"),
                                         masks[bass.ds(g.n, 1)].rearrange("g p s b n -> p (g s b) n"))\
                                .then_inc(mask_in, 16)
                            if g.start + 1 < G:
                                wait_apart(sp, ctx_split, g.n + 1)
                                load_ctx(g.n + 1)
                            r = g.start % 2
                            for half in range(2):
                                wait_apart(sp, stack_in[r][half], 16 * STACK_DMAS * round_of(g))
                            for n in range(4):
                                wait_apart(sp, parts_done, 4 * g.n + n + 1)
                                side, m = n // 2, n % 2
                                sp.dma_start(part_scr[r, side, :, m * P:(m + 1) * P, :].rearrange("a p n -> p a n"),
                                             parts[:, n]).then_inc(parts_stored, 16)

                    load_x(0, 0)
                    load_ctx(0)
                    for r in range(2):
                        for t, a, b in ((q_stack[r], 6 * HD, 6 * HD + PARTS), (k_stack[r], 6 * HD + PARTS, SCORE_ROWS_M)):
                            sp.dma_start(t[a:b].rearrange("p h n -> p (h n)"), ones[0:b - a, :]).then_inc(ones_in, 16)
                    pipeline(sp, step)
                    for r in range(2):
                        for half in range(2):
                            sp.wait_ge(stack_in[r][half], 16 * STACK_DMAS * G // 2)
                    for b in range(GB):
                        sp.wait_ge(max_in[b], 16 * G)

                @block.gpsimd
                def _(pool):
                    for r in range(2):
                        nc.gpsimd.memset(values[r][:], 1.0).then_inc(ones_ready, 1)

                    def split_max(g, b):
                        n = 4 * g.n + b + 1
                        nm, t = neg_max[:, b, :], m_tmp[:, b]
                        wait_apart(pool, slot_free[1], use(1, "max", g) + 2 * b + 2)
                        nc.gpsimd.tensor_scalar(t[:, 0], nm, 2.0 ** 40, None, ALU.mult).then_inc(m_over, 1)
                        wait_apart(pool, m_over, n)
                        nc.gpsimd.tensor_scalar(t[:, 1], t[:, 0], 0.0, None, ALU.mult).then_inc(m_zero, 1)
                        wait_apart(pool, m_zero, n)
                        nc.gpsimd.tensor_tensor(t[:, 2], nm, t[:, 1], ALU.add).then_inc(m_safe, 1)
                        wait_apart(pool, m_safe, n)
                        nc.gpsimd.tensor_copy(m_parts[:, b, 0], t[:, 2]).then_inc(m_hi, 1)
                        wait_apart(pool, m_hi, n)
                        nc.gpsimd.tensor_tensor(t[:, 3], t[:, 2], m_parts[:, b, 0], ALU.subtract).then_inc(m_rest, 1)
                        wait_apart(pool, m_rest, n)
                        nc.gpsimd.tensor_copy(m_parts[:, b, 1], t[:, 3]).then_inc(m_mid, 1)
                        wait_apart(pool, m_mid, n)
                        nc.gpsimd.tensor_tensor(m_parts[:, b, 2], t[:, 3], m_parts[:, b, 1], ALU.subtract)\
                            .then_inc(m_split, 1)

                    def step(maxima, attend, project, value):
                        if project:
                            norm_rstd(pool, project.n)
                        if maxima:
                            for b in range(GB):
                                split_max(maxima, b)
                        if project:
                            wait_apart(pool, ctx_high, project.n + 1)
                            nc.gpsimd.tensor_tensor(cl[:], ctx_raw[:], ch[:].bitcast(F32), ALU.subtract)\
                                .then_inc(ctx_split, 1)
                            for n in range(4):
                                wait_apart(pool, part2_done, 4 * project.n + n + 1)
                                nc.gpsimd.tensor_tensor(parts[:, n, 2], rest[:, n % 2], parts[:, n, 1], ALU.subtract)\
                                    .then_inc(parts_done, 1)

                    pipeline(pool, step)

                @block.scalar
                def _(act):
                    def exp(g, i):
                        act.wait_ge(slot_full[0], use(0, "exp", g) + i + 1)
                        if i >= 2:
                            act.wait_ge(pv_full, 8 * g.n + i - 1)
                        nc.scalar.activation(exps[i % 2][:].rearrange("p h n -> p (h n)"),
                                             SLOT[0].rearrange("p a n -> p (a n)"), ACT.Exp).then_inc(slot_free[0], 1)

                    def take_rows(g, b):
                        act.wait_ge(turn_full, turn_at("rows", g, b) + 1)
                        wait(act, max_stored[b], 16 * g.n)
                        nc.scalar.activation(max_rows[:, b, :], TURN.bitcast(BF16)[0:PARTS * HEADS, 0:P],
                                             ACT.Copy).then_inc(turn_free, 1)

                    def take_values(g, c):
                        bank_is_full(act, 1, "value", g, c)
                        out_ = nc.scalar.activation(values[g.start % 2][:, 2 * c:2 * c + 2, :, 0:HD],
                                                    SLOT[1][:, c, :].rearrange("p (b h d) -> p b h d", b=2, h=HEADS),
                                                    ACT.Copy)
                        if c == 1:
                            out_.then_inc(slot_free[1], 1)

                    def first_part(g, n):
                        if n < 2:
                            bank_is_full(act, 0, "query", g, n)
                        else:
                            act.wait_ge(pair_full[n - 2], at(pair_table, "key", g) + 1)
                        src = SLOT[0][:, n, :] if n < 2 else PAIR_BANK[n - 2]
                        nc.scalar.activation(parts[:, n, 0], src, ACT.Copy,
                                             scale=HD ** -0.5 if n < 2 else 1.0).then_inc(part1_done, 1)

                    def second_part(g, n):
                        s, count = ((rest_done, g.n), (slot_free[0], use(0, "query", g)),
                                    *((pair_free[m], at(pair_table, "key", g)) for m in range(2)))[n]
                        act.wait_ge(s, count + 1)
                        nc.scalar.activation(parts[:, n, 1], rest[:, n % 2], ACT.Copy).then_inc(part2_done, 1)

                    def step(maxima, attend, project, value):
                        for i in range(2 * GB):
                            if attend:
                                exp(attend, i)
                            if maxima and i in (3, 5, 7):
                                take_rows(maxima, (i - 3) // 2)
                        if project:
                            for c in range(2):
                                bank_is_full(act, 0, "turn_x", project, c)
                                nc.scalar.activation(xh[:, c, :], SLOT[0][:, c, :], ACT.Copy).then_inc(x_high, 1)
                        if value:
                            if value.start < 2:
                                act.wait_ge(ones_ready, 2)
                            take_values(value, 0)
                        if maxima:
                            take_rows(maxima, GB - 1)
                        if attend:
                            for c in range(2):
                                act.wait_ge(pair_full[c], at(pair_table, "attn", attend) + 1)
                                nc.scalar.activation(ah[:, c, :], PAIR_BANK[c], ACT.Copy).then_inc(a_high, 1)
                        if value:
                            take_values(value, 1)
                        if project:
                            act.wait_ge(ctx_in, 16 * (project.n + 1))
                            nc.scalar.activation(ch[:], ctx_raw[:], ACT.Copy).then_inc(ctx_high, 1)
                            wait(act, parts_stored, 64 * project.n)
                            for n in range(4):
                                first_part(project, n)
                                if n:
                                    second_part(project, n - 1)
                            second_part(project, 3)

                    pipeline(act, step)

                @block.vector
                def _(dve):
                    dve.wait_ge(fin_free, 8)
                    turned = TURN.rearrange("p (h v) -> p h v", v=VW)

                    def reduce_max(g, i):
                        b, s = divmod(i, 2)
                        dve.wait_ge(slot_full[1], use(1, "max", g) + i + 1)
                        nc.vector.tensor_reduce(neg_max[:, b, s * HH:(s + 1) * HH],
                                                SLOT[1].rearrange("p a (h n) -> p (a h) n", n=P),
                                                AX_X, ALU.max, negate=True).then_inc(slot_free[1], 1)

                    def take_heads(g, b):
                        dve.wait_ge(pv_full, 8 * g.n + 2 * b + 2)
                        nc.vector.tensor_copy(heads_t[b % 2][:], PV).then_inc(pv_free, 1)

                    def normalise(g, b):
                        n = 4 * g.n + b + 1
                        dve.wait_ge(turn_full, turn_at("heads", g, b) + 1)
                        nc.vector.tensor_scalar(den[:, b % 2], turned[:, :, HD], 1.0, None, ALU.add)\
                            .then_inc(den_done, 1)
                        dve.wait_ge(den_done, n)
                        nc.vector.reciprocal(recip[:, b % 2], den[:, b % 2]).then_inc(recip_done, 1)
                        dve.wait_ge(recip_done, n)
                        nc.vector.tensor_tensor(attn[:, b].rearrange("p (h d) -> p h d", d=HD), turned[:, :, 0:HD],
                                                recip[:, b % 2][:, :, None].to_broadcast([P, HEADS, HD]),
                                                ALU.mult).then_inc(turn_free, 1)

                    def make_rest(g, n):
                        dve.wait_ge(part1_done, 4 * g.n + n + 1)
                        wait(dve, parts_done, 4 * g.n + n - 1)
                        src = SLOT[0][:, n, :] if n < 2 else PAIR_BANK[n - 2]
                        nc.vector.scalar_tensor_tensor(rest[:, n % 2], src, HD ** -0.5 if n < 2 else 1.0,
                                                       parts[:, n, 0], ALU.mult, ALU.subtract)\
                            .then_inc((rest_done, slot_free[0], *pair_free)[n], 1)

                    def step(maxima, attend, project, value):
                        if project:
                            dve.wait_ge(x_in[project.start % 2], 16 * (round_of(project) + 1))
                            norm_measure(dve, project.n, project.n)
                        for i in range(2 * GB):
                            if attend and i >= 3 and i % 2:
                                normalise(attend, (i - 3) // 2)
                            if maxima:
                                reduce_max(maxima, i)
                            if attend and i >= 2 and i % 2 == 0:
                                take_heads(attend, i // 2 - 1)
                            if project and i == 2:
                                norm_apply(dve, project.n, project.n)
                        if attend:
                            take_heads(attend, GB - 1)
                            normalise(attend, GB - 1)
                        if project:
                            for c in range(2):
                                dve.wait_ge(x_high, 2 * project.n + c + 1)
                                low = nc.vector.tensor_tensor(xl[:, c, :], SLOT[0][:, c, :], xh[:, c, :].bitcast(F32),
                                                              ALU.subtract)
                                if c == 1:
                                    low.then_inc(slot_free[0], 1)
                        if attend:
                            for c in range(2):
                                dve.wait_ge(a_high, 2 * attend.n + c + 1)
                                nc.vector.tensor_tensor(al[:, c, :], PAIR_BANK[c], ah[:, c, :].bitcast(F32),
                                                        ALU.subtract).then_inc(pair_free[c], 1)
                        if value:
                            dve.wait_ge(mask_in, 16 * (value.n + 1))
                            nc.vector.tensor_scalar(mask_add[value.start % 2][:], mask_raw[:], 0.0, MASKED,
                                                    ALU.is_equal, ALU.mult).then_inc(mask_ready, 1)
                        if project:
                            for n in range(2):
                                make_rest(project, n)
                        if attend:
                            for c in range(2):
                                bank_is_full(dve, 1, "output", attend, c)
                                xg = x_all[:, bass.ds(GB * attend.n + 2 * c, 2), :].rearrange("p b n -> p (b n)")
                                out_ = nc.vector.tensor_tensor(xg, SLOT[1][:, c, :], xg, ALU.add)
                                if c == 1:
                                    out_.then_inc(slot_free[1], 1)
                        if project:
                            for n in range(2, 4):
                                make_rest(project, n)

                    pipeline(dve, step)

                @block.tensor
                def _(pe):
                    pe.wait_ge(fin_free, 8)
                    pe.wait_ge(w_split, 1)

                    def score_half(slot, count, r, i, rows, transposed):
                        b, s = divmod(i, 2)
                        wait(pe, slot_free[slot], count)
                        keep, move = (k_stack[r], q_stack[r]) if transposed else (q_stack[r], k_stack[r])
                        tok = slice(b * P, (b + 1) * P)
                        for q in range(2):
                            dst = SLOT[slot][:, q, :]
                            nc.tensor.matmul(dst.rearrange("p (h n) -> p h n", n=P), ident_bf[:, :],
                                             mask_add[r][:, int(transposed), b:b + 1, :].to_broadcast([P, 4, P]),
                                             start=True, stop=False, skip_group_check=True)
                            for j in range(4):
                                h = s * HH + 4 * q + j
                                last = nc.tensor.matmul(dst[:, j * P:(j + 1) * P], keep[0:rows, h, tok],
                                                        move[0:rows, h, tok], start=False, stop=(j == 3),
                                                        skip_group_check=True)
                        last.then_inc(slot_full[slot], 1)

                    def weigh(g, i):
                        b, s = divmod(i, 2)
                        pe.wait_ge(slot_free[0], use(0, "exp", g) + i + 1)
                        if s == 0 and b:
                            pe.wait_ge(pv_free, 4 * g.n + b)
                        for k in range(HH):
                            h = s * HH + k
                            j = k % 4
                            last = nc.tensor.matmul(PV[VW * j:VW * (j + 1), (h // 4) * P:(h // 4 + 1) * P],
                                                    values[g.start % 2][:, b, h, :], exps[s][:, k, :], start=True, stop=True)
                        last.then_inc(pv_full, 1)

                    def turn_heads(g, b):
                        pe.wait_ge(pv_free, 4 * g.n + b + 1)
                        wait(pe, turn_free, turn_at("heads", g, b))
                        for q in range(4):
                            last = nc.tensor.transpose(TURN[:, q * P:(q + 1) * P],
                                                       heads_t[b % 2][:, q * P:(q + 1) * P], ident[:, :])
                        last.then_inc(turn_full, 1)

                    def turn_attn(g, b):
                        pe.wait_ge(turn_free, turn_at("heads", g, b) + 1)
                        for c in range(2):
                            if b == 0:
                                wait(pe, pair_free[c], at(pair_table, "attn", g))
                            last = nc.tensor.transpose(PAIR_BANK[c][:, b * P:(b + 1) * P],
                                                       attn[:, b, c * P:(c + 1) * P], ident[:, :])
                            if b == GB - 1:
                                last.then_inc(pair_full[c], 1)

                    def turn_max(g, b):
                        pe.wait_ge(m_split, 4 * g.n + b + 1)
                        wait_apart(pe, turn_free, turn_at("rows", g, b))
                        nc.tensor.transpose(TURN.bitcast(BF16)[0:PARTS * HEADS, 0:P],
                                            m_parts[:, b].rearrange("p a h -> p (a h)"), ident_bf[:, :])\
                            .then_inc(turn_full, 1)

                    def split_product(dst, pairs, first_in_bank):
                        terms = [(l, r_) for (lh, ll), (rh, rl) in pairs for l, r_ in ((lh, rh), (ll, rh), (lh, rl))]
                        for i, (l, r_) in enumerate(terms):
                            last = nc.tensor.matmul(dst, l, r_, start=(first_in_bank and i == 0),
                                                    stop=(i == len(terms) - 1), skip_group_check=True)
                        return last

                    def tokens_product(name, g, c, a_h, a_l, w):
                        if c == 0:
                            wait(pe, slot_free[1], use(1, name, g))
                        for j in range(2):
                            tok = slice((2 * c + j) * P, (2 * c + j + 1) * P)
                            last = split_product(SLOT[1][:, c, j * DM:(j + 1) * DM],
                                                 [((a_h[:, k, tok], a_l[:, k, tok]), (wah[:, w, k, :], wal[:, w, k, :]))
                                                  for k in range(KD)], j == 0)
                        last.then_inc((half_full, slot_full)[c][1], 1)

                    def projection(dst, m, w, a_h, a_l):
                        cols = slice(m * P, (m + 1) * P)
                        return split_product(dst, [((wah[:, w, k, cols], wal[:, w, k, cols]), (a_h[:, k, :], a_l[:, k, :]))
                                                   for k in range(KD)], True)

                    def turn_tokens(g):
                        pe.wait_ge(xn_done, g.n + 1)
                        wait(pe, slot_free[0], use(0, "turn_x", g))
                        for c in range(2):
                            for b in range(GB):
                                last = nc.tensor.transpose(SLOT[0][:, c, b * P:(b + 1) * P], xn[:, b, c * P:(c + 1) * P],
                                                           ident[:, :])
                            last.then_inc((half_full, slot_full)[c][0], 1)

                    def step(maxima, attend, project, value):
                        if maxima:
                            pe.wait_ge(ones_in, 64)
                            pe.wait_ge(mask_ready, maxima.n + 1)
                        for i in range(2 * GB + 3):
                            b, s = divmod(i, 2)
                            if attend and i < 2 * GB:
                                if s == 0:
                                    pe.wait_ge(max_in[b], 16 * (attend.n + 1))
                                score_half(0, use(0, "exp", attend) + i, attend.start % 2, i, SCORE_ROWS_M, True)
                            if attend and s == 1 and b >= 1:
                                turn_heads(attend, b - 1)
                            if attend and s == 0 and b >= 2:
                                turn_attn(attend, b - 2)
                            if maxima and i < 2 * GB:
                                if i % GB == 0:
                                    pe.wait_ge(stack_in[maxima.start % 2][i // GB], 16 * STACK_DMAS * (round_of(maxima) + 1))
                                score_half(1, use(1, "max", maxima) + i, maxima.start % 2, i, SCORE_ROWS, False)
                            if value and i > 2 * GB:
                                tokens_product("value", value, i - 2 * GB - 1, ch, cl, 2)
                            if maxima and s == 1 and b >= 1:
                                turn_max(maxima, b - 1)
                            if attend and 1 <= i <= 2 * GB:
                                weigh(attend, i - 1)
                            if project and i == 2 * GB:
                                turn_tokens(project)
                        if project:
                            pe.wait_ge(slot_free[0], use(0, "query", project))
                            for m in range(2):
                                projection(SLOT[0][:, m, :], m, 0, xh, xl).then_inc((half_full, slot_full)[m][0], 1)
                        if attend:
                            for c in range(2):
                                pe.wait_ge(pair_free[c], at(pair_table, "attn", attend) + 1)
                            for c in range(2):
                                tokens_product("output", attend, c, ah, al, 3)
                        if project:
                            pe.wait_ge(ctx_split, project.n + 1)
                            for m in range(2):
                                wait(pe, pair_free[m], at(pair_table, "key", project))
                                projection(PAIR_BANK[m], m, 1, ch, cl).then_inc(pair_full[m], 1)

                    pipeline(pe, step)

        w1 = sb("w1", [P, KD, HID])
        w2 = sb("w2", [P, HC, DM])
        w1h = sb("w1h", [P, KD, HID], F32R)
        w1l = sb("w1l", [P, KD, HID], F32R)
        w2h = sb("w2h", [P, HC, DM], F32R)
        w2l = sb("w2l", [P, HC, DM], F32R)
        gh = sb("gh", [P, 2, GT], F32R)
        gl = sb("gl", [P, 2, GT], F32R)
        gf = sb("gf", [P, 2, GT])
        x_res = sb("x_res", [P, GB, DM])
        y_out = sb("y_out", [P, GB, DM])
        T = [psum[:, c, :] for c in range(2)]
        HB = [psum[:, 2 + i, :] for i in range(2)]
        Y = [psum[:, 4 + c, :] for c in range(2)]

        def weight_pieces():
            for q in range(4):
                yield tuple(t[:, :, q * DM:(q + 1) * DM] for t in (w1, w1h, w1l))
                yield tuple(t[:, 2 * q:2 * q + 2, :] for t in (w2, w2h, w2l))

        with nc.Block() as block:
            @block.sync
            def _(sp):
                sp.dma_start(w1[:], w1_scr).then_inc(w1_in, 16)
                sp.dma_start(w2[:], w2_scr).then_inc(w2_in, 16)
                with sp.Fori(0, G) as g:
                    wait_apart(sp, y_done, 2 * g + 2)
                    sp.dma_start(out[bass.ds(GB * g, GB)].rearrange("b p n -> p b n"), y_out[:]).then_inc(stored, 16)
                sp.wait_ge(stored, 16 * G)

            @block.gpsimd
            def _(pool):
                def residual(g):
                    wait_apart(pool, stored, 16 * g)
                    nc.gpsimd.tensor_tensor(x_res[:], x_all[:, bass.ds(GB * g, GB), :],
                                            bias_sum[:, None, :].to_broadcast([P, GB, DM]), ALU.add)\
                        .then_inc(res_ready, 1)

                norm_rstd(pool, G)
                residual(0)
                with pool.Fori(1, G) as g:
                    norm_rstd(pool, g + G)
                    residual(g)

            @block.scalar
            def _(act):
                def take_tokens(g):
                    for c in range(2):
                        act.wait_ge(t_full[c], g + 1)
                        nc.scalar.activation(xh[:, c, :], T[c], ACT.Copy).then_inc(t_high, 1)

                def hidden(g):
                    for c in range(HC):
                        act.wait_ge(h_full, 8 * g + c + 1)
                        if c >= 2:
                            act.wait_ge(ffn_used, 8 * g + c - 1)
                        nc.scalar.activation(gf[:, c % 2], HB[c % 2], ACT.Gelu, bias=hid_bias[:, c:c + 1])
                        nc.scalar.activation(gh[:, c % 2], HB[c % 2], ACT.Gelu, bias=hid_bias[:, c:c + 1])\
                            .then_inc(g_done, 1)

                take_tokens(0)
                for n, (whole, high, low) in enumerate(weight_pieces()):
                    if n < 2:
                        act.wait_ge((w1_in, w2_in)[n], 16)
                    nc.scalar.activation(high, whole, ACT.Copy).then_inc(wffn_high, 1)
                with act.Fori(0, G - 1) as g:
                    hidden(g)
                    take_tokens(g + 1)
                hidden(G - 1)

            @block.vector
            def _(dve):
                def split_tokens(g):
                    for c in range(2):
                        dve.wait_ge(t_high, 2 * g + c + 1)
                        nc.vector.tensor_tensor(xl[:, c, :], T[c], xh[:, c, :].bitcast(F32), ALU.subtract)\
                            .then_inc(t_free[c], 1)

                def hidden(g, chunks):
                    for c in chunks:
                        dve.wait_ge(g_done, 8 * g + c + 1)
                        nc.vector.tensor_tensor(gl[:, c % 2], gf[:, c % 2], gh[:, c % 2].bitcast(F32), ALU.subtract)\
                            .then_inc(g_split, 1)

                def finish(g):
                    dve.wait_ge(res_ready, g + 1)
                    dve.wait_ge(ffn_used, 8 * g + 8)
                    for c in range(2):
                        nc.vector.tensor_tensor(y_out[:, 2 * c:2 * c + 2].rearrange("p b n -> p (b n)"), Y[c],
                                                x_res[:, 2 * c:2 * c + 2].rearrange("p b n -> p (b n)"), ALU.add)\
                            .then_inc(y_done, 1)

                norm_measure(dve, 0, G)
                norm_apply(dve, 0, G)
                split_tokens(0)
                for n, (whole, high, low) in enumerate(weight_pieces()):
                    if n < 2:
                        dve.wait_ge((w1_in, w2_in)[n], 16)
                    dve.wait_ge(wffn_high, n + 1)
                    nc.vector.tensor_tensor(low, whole, high.bitcast(F32), ALU.subtract).then_inc(wffn_split, 1)
                with dve.Fori(0, G - 1) as g:
                    hidden(g, range(2))
                    norm_measure(dve, g + 1, g + 1 + G)
                    hidden(g, range(2, 5))
                    norm_apply(dve, g + 1, g + 1 + G)
                    hidden(g, range(5, HC))
                    split_tokens(g + 1)
                    finish(g)
                hidden(G - 1, range(HC))
                finish(G - 1)

            @block.tensor
            def _(pe):
                def turn_tokens(g):
                    pe.wait_ge(xn_done, g + 1 + G)
                    for c in range(2):
                        wait(pe, t_free[c], g)
                        for b in range(GB):
                            last = nc.tensor.transpose(T[c][:, b * P:(b + 1) * P], xn[:, b, c * P:(c + 1) * P],
                                                       ident[:, :])
                        last.then_inc(t_full[c], 1)

                def up(g, c):
                    pe.wait_ge(wffn_split, 2 * (c // 2) + 1)
                    if c >= 2:
                        pe.wait_ge(g_done, 8 * g + c - 1)
                    n = 0
                    cols = slice(c * P, (c + 1) * P)
                    for k in range(KD):
                        for w, t in ((w1h, xh), (w1l, xh), (w1h, xl)):
                            last = nc.tensor.matmul(HB[c % 2], w[:, k, cols], t[:, k, :], start=(n == 0),
                                                    stop=(n == 5))
                            n += 1
                    last.then_inc(h_full, 1)

                def down(g, c):
                    pe.wait_ge(g_split, 8 * g + c + 1)
                    pe.wait_ge(wffn_split, 2 * (c // 2) + 2)
                    for b in range(GB):
                        tok = slice(b * P, (b + 1) * P)
                        for i, (t, w) in enumerate(((gh, w2h), (gl, w2h), (gh, w2l))):
                            last = nc.tensor.matmul(Y[b // 2][:, (b % 2) * DM:(b % 2 + 1) * DM], t[:, c % 2, tok],
                                                    w[:, c, :], start=(c == 0 and i == 0 and b % 2 == 0),
                                                    stop=(c == HC - 1 and i == 2), skip_group_check=True)
                    last.then_inc(ffn_used, 1)

                def group_ffn(g, ahead):
                    for c in range(2):
                        pe.wait_ge(t_free[c], g + 1)
                    for c in range(HC):
                        up(g, c)
                        if c:
                            down(g, c - 1)
                    if ahead:
                        turn_tokens(g + 1)
                    down(g, HC - 1)

                turn_tokens(0)
                with pe.Fori(0, G - 1) as g:
                    group_ffn(g, True)
                group_ffn(G - 1, False)


def _mix_weights(w, np):
    out = np.empty((P, MIX_STAGES, HC // 2, 4), w.dtype)
    for k, _, _, pair in MIX_UP:
        out[:, k, pair] = w[BLOCK_STAGES + k, pair * P:(pair + 1) * P].reshape(P, 4)
    return out


def _block_factors(w, np):
    i = np.arange(P)[:, None, None, None]
    c = np.arange(HC)[None, :, None, None]
    out = []
    for k in range(BLOCK_STAGES):
        o = np.arange(2)[None, None, :, None]
        low = np.arange(2 ** k)[None, None, None, :]
        pair = (c * P + i >> (k + 1)) * 2 ** k + low
        out.append(w[k][pair, o, (i >> k) & 1].reshape(P, -1))
    return np.concatenate(out, 1)


def kernel(x, ctx_1024, itok_BxS_8_8191, itok_BxS2_1_8191, mask_BxSxS2_if1, L0_xattn_W_q, L0_xattn_W_k,
           L0_xattn_W_v, L0_xattn_W_o, L0_ffn_W_exp, L0_ffn_b_exp, L0_ffn_up_weights, L0_ffn_up_bias,
           L0_ffn_down_weights, L0_ffn_W_con, L0_ffn_b_con, L0_ffn_down_bias):
    import numpy as np
    import concourse.bacc as bacc
    from concourse.bass_utils import run_bass_kernel_spmd

    def arr(a):
        return np.asarray(a)

    mask = arr(mask_BxSxS2_if1).reshape(G, GB, P, P)
    pos = np.stack([arr(itok_BxS_8_8191), arr(itok_BxS2_1_8191)], 0).reshape(2, G, 1, GT)
    ratio = 2.0 ** (-8.0 / HEADS)
    slope = np.array([ratio ** i for i in range(1, HEADS + 1)], np.float32)

    def by_chunk(a):
        return a.reshape(-1, P, a.shape[-1]).transpose(1, 0, 2)

    def side_order(w):
        return w.T.reshape(DM, HEADS, HD).transpose(0, 2, 1).reshape(DM, DM)

    weights = [side_order(arr(L0_xattn_W_q)), side_order(arr(L0_xattn_W_k)), arr(L0_xattn_W_v).T, arr(L0_xattn_W_o).T]
    arrays = {
        "x": arr(x),
        "ctx_t": arr(ctx_1024).reshape(G, GT, KD, P).transpose(0, 3, 2, 1),
        "masks": np.stack([mask.transpose(0, 2, 1, 3), mask.transpose(0, 3, 1, 2)], 2),
        "pos": np.broadcast_to(pos, (2, G, HEADS, GT)).reshape(2, P, GT).transpose(1, 0, 2),
        "slopes": np.tile(np.stack([-slope, slope], 1), (G, 1)),
        "w_attn": np.stack([by_chunk(w) for w in weights], 1),
        "w_exp_t": by_chunk(np.concatenate([arr(L0_ffn_W_exp).T, arr(L0_ffn_b_exp)[:, None]], 1)),
        "w_con": by_chunk(arr(L0_ffn_W_con)),
        "up_bias": arr(L0_ffn_up_bias).reshape(HC, P).T,
        "out_bias": np.broadcast_to(np.stack([arr(L0_ffn_b_con), arr(L0_ffn_down_bias)]), (P, 2, DM)),
        "up_factors": _block_factors(arr(L0_ffn_up_weights), np),
        "down_factors": _block_factors(arr(L0_ffn_down_weights), np),
        "up_mix": _mix_weights(arr(L0_ffn_up_weights), np),
        "down_mix": _mix_weights(arr(L0_ffn_down_weights), np),
        "ones": np.ones((2 * PARTS, HEADS * GT), mybir.dt.np(BF16)),
    }
    arrays = {n: np.ascontiguousarray(a) for n, a in arrays.items()}
    nc = bacc.Bacc("TRN2", target_bir_lowering=False, num_devices=1)
    args = [nc.dram_tensor(f"in_{n}", a.shape, mybir.dt.from_np(a.dtype), kind="ExternalInput").ap()
            for n, a in arrays.items()]
    args.append(nc.dram_tensor("out_x", (BATCHES, P, DM), F32, kind="ExternalOutput").ap())
    build(nc, *args)
    r = run_bass_kernel_spmd(nc, [{f"in_{n}": a for n, a in arrays.items()}], core_ids=[0])
    return r.results[0]["out_x"]
```

```python
from collections import namedtuple
from functools import partial
from contextlib import ExitStack

import concourse.bass as bass
from concourse import mybir

ALU = mybir.AluOpType
ACT = mybir.ActivationFunctionType
AX_X = mybir.AxisListType.X
F32 = mybir.dt.float32
F32R = mybir.dt.float32r
BF16 = mybir.dt.bfloat16
I32 = mybir.dt.int32

P = 128
BATCHES = 32
DM = 256
KD = DM // P
HEADS, HD = 16, 16
HID = 1024
HC = HID // P
GB = 4
G = BATCHES // GB
GT = GB * P
BLOCK_STAGES = 7
MIX_STAGES = 3
PARTS = 3
HH = 8
VW = 32
EPS = 1e-5
MASKED = -(2.0 ** 100)
SCORE_ROWS = 6 * HD + 2 * PARTS
SCORE_ROWS_M = SCORE_ROWS + PARTS
HID_BUFS = 4
LAG = 2
MIX_TMP = 2
STACK_DMAS = 8

FACTOR_AT = [HC * (2 ** (k + 1) - 2) for k in range(BLOCK_STAGES)]
FACTOR_N = HC * (2 ** (BLOCK_STAGES + 1) - 2)
MIX_UP = [(k, blk * 2 * s + sub, blk * 2 * s + sub + s, blk * s + sub)
          for k, s in enumerate((1, 2, 4)) for blk in range(HC // (2 * s)) for sub in range(s)]
MIX_DOWN = [x for k in (2, 1, 0) for x in MIX_UP if x[0] == k]


def build(nc, x, ctx_t, masks, pos, slopes, w_attn, w_exp_t, w_con, up_bias, out_bias,
          up_factors, down_factors, up_mix, down_mix, ones, out):
    part_scr = nc.dram_tensor("part_scr", (2, 2, PARTS, DM, GT), BF16).ap()
    pos_scr = nc.dram_tensor("pos_scr", (2, PARTS, P, GT), BF16).ap()
    max_scr = nc.dram_tensor("max_scr", (GB, PARTS * HEADS, P), BF16).ap()

    with ExitStack() as stack:
        def sb(name, shape, dt=F32):
            return stack.enter_context(nc.sbuf_tensor(name, shape, dt))

        def sem(name):
            return stack.enter_context(nc.semaphore(name))

        def region(name, *lives):
            tensors, size = [], 0
            for n, life in enumerate(lives):
                words = 0
                with ExitStack() as at_start:
                    for m, (shape, dt) in enumerate(life):
                        tensors.append(at_start.enter_context(nc.sbuf_tensor(f"{name}_{n}_{m}", [P, *shape], dt)))
                        count = 1
                        for d in shape:
                            count *= d
                        words += count // 2 if dt == BF16 else count
                size = max(size, words)
            sb(name, [P, size])
            return tensors

        ident = sb("ident", [P, P])
        ident_bf = sb("ident_bf", [P, P], BF16)
        x_all = sb("x_all", [P, BATCHES, DM])
        hid_bias = sb("hid_bias", [P, HC])
        upb = sb("upb", [P, HC])
        bias_sum = sb("bias_sum", [P, DM])
        mixw = [sb(f"mixw{d}", [P, MIX_STAGES, HC // 2, 4]) for d in range(2)]
        neg_half = sb("neg_half", [P, GB])
        stats = sb("stats", [P, GB, 6])
        mean_var = sb("mean_var", [P, GB, 2])
        var_eps = sb("var_eps", [P, GB])
        rstd = sb("rstd", [P, GB])
        row_least = sb("row_least", [P, 1])
        row_masked = sb("row_masked", [P, 1])
        masked = sb("masked", [P, GB], I32)
        mask_squares = x_all[:, BATCHES // 2:, :].rearrange("p b n -> p (b n)")
        all_masks = mask_squares.bitcast(I32)
        w_oh = sb("w_oh", [P, KD, DM], F32R)
        w_ol = sb("w_ol", [P, KD, DM], F32R)
        mask_add = [sb(f"mask_add{r}", [P, 2, GB, P], BF16) for r in range(2)]
        neg_max = sb("neg_max", [P, GB, HEADS])
        m_tmp = sb("m_tmp", [P, GB, 4, HEADS])
        m_parts = sb("m_parts", [P, GB, PARTS, HEADS], BF16)
        max_rows = sb("max_rows", [PARTS * HEADS, GB, P], BF16)
        exps = [sb(f"exps{s}", [P, HH, P]) for s in range(2)]
        ah = sb("ah", [P, KD, GT], F32R)
        al = sb("al", [P, KD, GT], F32R)
        heads_t = [sb(f"heads_t{i}", [P, 512]) for i in range(2)]
        den = sb("den", [P, 2, HEADS])
        recip = sb("recip", [P, 2, HEADS])
        attn = sb("attn", [P, GB, DM])
        values_1 = sb("values1", [P, GB, HEADS, VW])
        mix_tmp = sb("mix_tmp", [P, MIX_TMP, DM + 1])
        tokens = ((KD, GT), F32R)
        weight = ((KD, DM), F32R)
        (xn, xh, xl, rest, ctx_raw, parts, w_qh, w_ql, w_kh, w_kl,
         mix_spare, down_a, factors, wet, block0, block1) = region(
            "project_mem",
            [((GB, DM), F32), tokens, tokens, ((2, GT), F32), ((KD, GT), F32), ((4, PARTS, GT), BF16), *[weight] * 4],
            [((HC, DM + 1), F32), ((HC, DM), F32), ((FACTOR_N,), F32), ((HC, DM + 1), F32), *[((HC, P), F32)] * 2])
        blocks = [block0, block1]
        (w_vh, w_vl, ch, cl, mask_raw, w1h, w1l) = region(
            "value_mem", [weight, weight, tokens, tokens, ((2, GB, P), I32)], [((KD, HID), F32R)] * 2)
        stack_ = ((HEADS, GT), BF16)
        (q_stack_0, k_stack_0, values_0, w2h, w2l, gh, gl) = region(
            "attend_mem", [stack_, stack_, ((GB, HEADS, VW), F32)],
            [*[((HC, DM), F32R)] * 2, *[((HID_BUFS, GT), F32R)] * 2])
        (q_stack_1, k_stack_1, wa, posi, posf, posr, posp, slope, outb, gf, x_res, y_out) = region(
            "odd_stack_mem", [stack_, stack_],
            [((4, KD, DM), F32), ((2, GT), I32), ((2, GT), F32), ((2, GT), F32), ((2, PARTS, GT), BF16), ((2,), F32),
             ((2, DM), F32)],
            [((HID_BUFS, GT), F32), *[((GB, DM), F32)] * 2])
        w_high_part = [w_qh, w_kh, w_vh, w_oh]
        w_low_part = [w_ql, w_kl, w_vl, w_ol]
        q_stack, k_stack, values = [q_stack_0, q_stack_1], [k_stack_0, k_stack_1], [values_0, values_1]

        psum = stack.enter_context(nc.psum_tensor("psum", [P, 8, 512], F32))

        wa_in = [sem(f"wa_in{w}") for w in range(4)]
        pos_in = sem("pos_in")
        all_masks_in, squares_done, least_found, rows_found, masked_full, masked_ready = (
            sem(n) for n in ("all_masks_in", "squares_done", "least_found", "rows_found", "masked_full", "masked_ready"))
        small_in = sem("small_in")
        wc_in = sem("wc_in")
        wet_in = sem("wet_in")
        factors_in = sem("factors_in")
        waits_passed = sem("waits_passed")
        x_in = [sem(f"x_in{r}") for r in range(2)]
        ctx_in = sem("ctx_in")
        mask_in = sem("mask_in")
        ident_ready = sem("ident_ready")
        ones_ready = sem("ones_ready")
        ones_in = [sem(f"ones_in{r}") for r in range(2)]
        w_high = sem("w_high")
        w_split = sem("w_split")
        pos_val, pos_hi, pos_rest, pos_mid, pos_split = (sem(f"pos_{n}") for n in ("val", "hi", "rest", "mid", "split"))
        pos_stored = sem("pos_stored")
        grow = sem("grow")
        pre_full = sem("pre_full")
        pre_free = sem("pre_free")
        mix_first = sem("mix_first")
        mix_out = sem("mix_out")
        made_full = sem("made_full")
        made_high = sem("made_high")
        made_free = sem("made_free")
        bias_ready = sem("bias_ready")
        stats_done, var_done, eps_done, rstd_done, xn_done = (
            sem(f"{n}_done") for n in ("stats", "var", "eps", "rstd", "xn"))
        bank_full = [[sem(f"bank_full{s}{c}") for c in range(2)] for s in range(2)]
        bank_free = [[sem(f"bank_free{s}{c}") for c in range(2)] for s in range(2)]
        pair_full = [sem(f"pair_full{c}") for c in range(2)]
        pair_free = [sem(f"pair_free{c}") for c in range(2)]
        turn_full = sem("turn_full")
        turn_free = sem("turn_free")
        pv_full = sem("pv_full")
        pv_free = sem("pv_free")
        x_high, a_high, ctx_high = (
            sem(n) for n in ("x_high", "a_high", "ctx_high"))
        ctx_split = [sem(f"ctx_split{c}") for c in range(2)]
        part1_done, part2_done, parts_done = (
            sem(n) for n in ("part1_done", "part2_done", "parts_done"))
        parts_stored = [sem(f"{side}_parts_stored") for side in ("q", "k")]
        mask_ready = sem("mask_ready")
        stack_in = [[sem(f"stack_in{r}{half}") for half in range(2)] for r in range(2)]
        m_over, m_zero, m_safe, m_hi, m_rest, m_mid, m_split = (
            sem(n) for n in ("m_over", "m_zero", "m_safe", "m_hi", "m_rest", "m_mid", "m_split"))
        max_stored = [sem(f"max_stored{b}") for b in range(GB)]
        max_in = [sem(f"max_in{b}") for b in range(GB)]
        den_done = sem("den_done")
        recip_done = sem("recip_done")
        t_full = [sem(f"t_full{c}") for c in range(2)]
        t_free = [sem(f"t_free{c}") for c in range(2)]
        t_high = sem("t_high")
        h_full = sem("h_full")
        g_done = sem("g_done")
        g_split = sem("g_split")
        ffn_used = sem("ffn_used")
        res_ready = sem("res_ready")
        y_done = sem("y_done")
        stored = sem("stored")

        Group = namedtuple("Group", "n start turn")
        FIRST_STEP, LOOP_STEP, LOOP_TURNS, LAST_STEP = -2, 1, 2, G
        BUTTERFLIES = {G - 2: "down mixes", G - 1: "up mixes", G: "products"}

        def stages(step):
            return [g if 0 <= g < G else None for g in (step, step - 1, step + 2, step + 1)]

        SCORE_T = [("exp", 1, 2 * GB), ("max", 0, 0), ("turn_x", 2, 1), ("query", 2, 1)]
        SCORE = [("max", 0, 2 * GB), ("value", 3, 1), ("output", 1, 1)]
        PAIR = [("key", 3, 1), ("attn", 1, 1)]

        def counts(uses):
            table, done = {}, 0
            for step in range(FIRST_STEP, LAST_STEP + 1):
                for name, stage, number in uses:
                    g = stages(step)[stage]
                    if g is not None:
                        table[name, g] = done
                        done += GB if (name, g) == ("max", 0) else number
            return table

        slot_table = [counts(SCORE_T), counts(SCORE)]
        pair_table = counts(PAIR)
        turn_table, turned = {}, 0
        for step in range(FIRST_STEP, LAST_STEP + 1):
            here = [(n, g) for n, g in zip(("rows", "heads"), stages(step)) if g is not None]
            for n, g in here:
                turn_table[n, g] = (turned + (len(here) == 2 and n == "rows"), len(here))
            turned += GB * len(here)

        def at(table, name, g):
            value = table[name, g.start]
            if isinstance(g.turn, int) and g.turn == 0 and isinstance(g.n, int):
                return value
            by = table[name, g.start + 2] - value
            return value + by * g.turn

        def turn_at(name, g, b):
            first, by = turn_table[name, g.start]
            if isinstance(g.n, int):
                return first + by * b
            return first + by * b + 2 * GB * 2 * g.turn

        def wait(eng, s, value):
            if not (isinstance(value, int) and value <= 0):
                eng.wait_ge(s, value)

        def wait_apart(eng, s, value):
            if isinstance(value, int):
                wait(eng, s, value)
            else:
                eng.wait_ge(s, value)
                eng.sem_inc(waits_passed, 1)

        def groups(first, turn=0):
            return [None if g is None else Group(g + 2 * turn, g, turn) for g in stages(first)]

        def opening(step):
            for j in range(FIRST_STEP, 0):
                step(None, *groups(j))

        def pipeline(eng, step, begin=0):
            for j in range(begin, LOOP_STEP):
                step(None, *groups(j))
            with eng.Fori(0, LOOP_TURNS) as turn:
                step(None, *groups(LOOP_STEP, turn))
                step(None, *groups(LOOP_STEP + 1, turn))
            for j in range(LOOP_STEP + 2 * LOOP_TURNS, LAST_STEP + 1):
                step(BUTTERFLIES.get(j), *groups(j))

        def norm_stats(g, batches):
            xg = x_all[:, bass.ds(GB * g, GB), :]
            for b in batches:
                last = nc.vector.bn_stats(stats[:, b, :], xg[:, b, :])
                if b == GB - 1:
                    last.then_inc(stats_done, 1)

        def norm_measure(dve, n):
            wait_apart(dve, stats_done, n + 1)
            for b in range(GB):
                last = nc.vector.bn_aggr(mean_var[:, b, :], stats[:, b, :])
            last.then_inc(var_done, 1)

        def norm_apply(dve, g, n, batches=range(GB)):
            xg = x_all[:, bass.ds(GB * g, GB), :]
            if batches[0] == 0:
                dve.wait_ge(rstd_done, n + 1)
            for b in batches:
                last = nc.vector.tensor_scalar(xn[:, b, :], xg[:, b, :], mean_var[:, b, 0:1], rstd[:, b:b + 1],
                                               ALU.subtract, ALU.mult)
                if b == GB - 1:
                    last.then_inc(xn_done, 1)

        def norm_rstd(pool, n):
            wait_apart(pool, var_done, n + 1)
            nc.gpsimd.tensor_scalar(var_eps[:, :], mean_var[:, :, 1], EPS, None, ALU.add).then_inc(eps_done, 1)
            wait_apart(pool, eps_done, n + 1)
            nc.gpsimd.tensor_tensor(rstd[:, :], var_eps[:, :], neg_half[:, :], ALU.pow).then_inc(rstd_done, 1)

        T = [psum[:, c, :] for c in range(2)]

        def turn_ffn_tokens(pe, g):
            pe.wait_ge(xn_done, g + 1 + G)
            for c in range(2):
                wait(pe, t_free[c], g)
                for b in range(GB):
                    last = nc.tensor.transpose(T[c][:, b * P:(b + 1) * P], xn[:, b, c * P:(c + 1) * P], ident[:, :])
                last.then_inc(t_full[c], 1)

        def take_ffn_tokens(act, g):
            for c in range(2):
                act.wait_ge(t_full[c], g + 1)
                nc.scalar.activation(xh[:, c, :], T[c], ACT.Copy).then_inc(t_high, 1)

        def split_ffn_tokens(dve, g):
            for c in range(2):
                dve.wait_ge(t_high, 2 * g + c + 1)
                nc.vector.tensor_tensor(xl[:, c, :], T[c], xh[:, c, :].bitcast(F32), ALU.subtract)\
                    .then_inc(t_free[c], 1)

        def mixes():
            for d, (bufs, plan) in ((1, ([mix_spare[:, :, 0:DM], down_a], MIX_DOWN)), (0, ([mix_spare, wet], MIX_UP))):
                for n, (k, a, b, pair) in enumerate(plan):
                    src, dst = bufs[n // 4 % 2], bufs[1 - n // 4 % 2]
                    w = mixw[d][:, k, pair, :]
                    wa0, wb0, wa1, wb1 = (0, 1, 2, 3) if d == 0 else (0, 2, 1, 3)
                    yield src, dst, a, b, a, w[:, wa0:wa0 + 1], w[:, wb0:wb0 + 1]
                    yield src, dst, a, b, b, w[:, wa1:wa1 + 1], w[:, wb1:wb1 + 1]

        PRODUCT_TURNS = (0, 1, 3, 4, 6)
        all_mixes = list(enumerate(mixes()))
        N_MIX = len(all_mixes) // 2
        STAGE_MIX = N_MIX // MIX_STAGES

        DOWN_MIX_TURNS = (0, 0, 0, 0, 3, 8, 13, 19, 24)

        def mix_turn(butterfly, i):
            if butterfly == "down mixes":
                return all_mixes[DOWN_MIX_TURNS[i]:DOWN_MIX_TURNS[i + 1]]
            if butterfly == "up mixes":
                return all_mixes[N_MIX + 3 * i:N_MIX + 3 * (i + 1)]
            return []

        def mix_source_ready(eng, n):
            if n == 0:
                eng.wait_ge(small_in, 48)
                eng.wait_ge(wc_in, 16)
                eng.wait_ge(parts_done, 4 * G)
            elif n == N_MIX:
                eng.wait_ge(pre_free, HC // 2)
            elif n % STAGE_MIX == 0:
                eng.wait_ge(mix_out, n)

        last_block = (BLOCK_STAGES - 1) % 2

        SLOT = [psum[:, 0:2, :], psum[:, 2:4, :]]
        PV, TURN = psum[:, 4, :], psum[:, 5, :]
        PAIR_BANK = [psum[:, 6, :], psum[:, 7, :]]
        HALF_TOKENS = [slice(0, GT // 2), slice(GT // 2, GT)]

        flat = "p a b -> p (a b)"
        made_pieces = [(w1h[:, k, :], w1l[:, k, :]) for k in range(KD)]
        made_pieces += [(blocks[1 - last_block].rearrange(flat), None)]
        made_pieces += [tuple(w[:, c:c + HC // 2, :].rearrange(flat) for w in (w2h, w2l)) for c in (0, HC // 2)]

        def use(s, name, g):
            return at(slot_table[s], name, g)

        def max_use(g, i):
            return (i % 2, use(i % 2, "max", g) + i // 2) if g.start == 0 else (1, use(1, "max", g) + i)

        def bank_is_full(eng, s, name, g, c):
            eng.wait_ge(bank_full[s][c], use(s, name, g) + 1)

        def round_of(g):
            return g.start // 2 + g.turn

        with nc.Block() as block:
            @block.sync
            def _(sp):
                def load_x(g, n_round):
                    sp.dma_start(x_all[:, bass.ds(GB * g, GB), :],
                                 x[bass.ds(GB * g, GB)].rearrange("b p n -> p b n")).then_inc(x_in[n_round], 16)

                def load_ctx(g):
                    sp.dma_start(ctx_raw[:], ctx_t[bass.ds(g, 1)].rearrange("g p k n -> p (g k) n"))\
                        .then_inc(ctx_in, 16)

                def store_parts(g, pieces):
                    for n in pieces:
                        wait_apart(sp, parts_done, 4 * g.n + n + 1)
                        side, m = n // 2, n % 2
                        sp.dma_start(part_scr[g.start % 2, side, :, m * P:(m + 1) * P, :].rearrange("a p n -> p a n"),
                                     parts[:, n]).then_inc(parts_stored[side], 16)

                def store_max(g, b):
                    wait_apart(sp, turn_free, turn_at("rows", g, b) + 1)
                    sp.dma_start(max_scr[b], max_rows[:, b, :]).then_inc(max_stored[b], 16)

                def load_max(g, b):
                    wait_apart(sp, max_stored[b], 16 * (g.n + 1))
                    sp.dma_start(q_stack[g.start % 2][SCORE_ROWS:SCORE_ROWS_M, :, b * P:(b + 1) * P],
                                 max_scr[b].rearrange("(a h) n -> a h n", a=PARTS)).then_inc(max_in[b], 16)

                def load_stacks(g, attend, half):
                    r = g.start % 2
                    if half == 0:
                        if g.start == 0:
                            sp.wait_ge(pos_stored, 32)
                        if g.start == 1:
                            sp.wait_ge(w_split, 4)
                            load_ones(1)
                        for side in range(2):
                            wait_apart(sp, parts_stored[side], 32 * (g.n + 1))
                    if attend is not None:
                        wait_apart(sp, bank_full[0][1], use(0, "exp", attend) + GB * (half + 1))
                    tok = HALF_TOKENS[half]
                    for side, st, pieces in ((0, q_stack[r], [(0, 0, 3), (3, 0, 2), (5, 0, 1)]),
                                             (1, k_stack[r], [(0, 0, 3), (3, 1, 2), (5, 2, 1)])):
                        scr = part_scr[r, side].rearrange("a (i h) n -> (a i) h n", h=HEADS)
                        for row, part, n in pieces:
                            if side == 0 or n == 1:
                                src = scr[HD * part:HD * (part + n), :, tok]
                            else:
                                src = scr[None, HD * part:HD * (part + 1), :, tok].to_broadcast([n, HD, HEADS, GT // 2])
                            sp.dma_start(st[HD * row:HD * (row + n), :, tok], src).then_inc(stack_in[r][half], 16)
                        row = 6 * HD + (PARTS if side == 0 else 0)
                        sp.dma_start(st[row:row + PARTS, :, tok], pos_scr[side][:, bass.ds(HEADS * g.n, HEADS), tok])\
                            .then_inc(stack_in[r][half], 16)

                def step(butterfly, maxima, attend, project, value):
                    def with_max(store=None, load=None):
                        if maxima and store is not None:
                            store_max(maxima, store)
                        if maxima and load is not None:
                            load_max(maxima, load)

                    if attend:
                        store_max(attend, GB - 1)
                    if project and project.start + 1 < G:
                        load_x(project.n + 1, (project.start + 1) % 2)
                    if attend:
                        load_max(attend, GB - 1)
                    if value and value.start == G - 1:
                        sp.wait_ge(bank_full[0][1], use(0, "query", value) + 1)
                        sp.dma_start(mix_spare[:, :, 0:DM], w_con).then_inc(wc_in, 16)
                    if value:
                        store_parts(value, (2, 3))
                    if butterfly == "down mixes":
                        sp.wait_ge(parts_stored[1], 32 * G)
                        sp.dma_start(factors[:], up_factors).then_inc(factors_in, 16)
                        sp.dma_start(wet[:], w_exp_t).then_inc(wet_in, 16)
                    with_max(store=0)
                    if value:
                        load_stacks(value, attend, 0)
                    with_max(load=0)
                    with_max(store=1)
                    if value:
                        load_stacks(value, attend, 1)
                    with_max(load=1)
                    with_max(store=2)
                    g = project
                    if g:
                        wait_apart(sp, mask_ready, g.n)
                        sp.dma_start(mask_raw[:].rearrange("p s b n -> p (s b) n"),
                                     masks[bass.ds(g.n, 1)].rearrange("g p s b n -> p (g s b) n"))\
                            .then_inc(mask_in, 16)
                    with_max(load=2)
                    if g and g.start + 1 < G:
                        for half in range(2):
                            wait_apart(sp, ctx_split[half], g.n + 1)
                        load_ctx(g.n + 1)
                    if project and project.start == 0:
                        sp.wait_ge(pos_split, 1)
                        for side in range(2):
                            sp.dma_start(pos_scr[side].rearrange("a p n -> p a n"), posp[:, side]).then_inc(pos_stored, 16)
                    if g:
                        r = g.start % 2
                        for half in range(2):
                            wait_apart(sp, stack_in[r][half], 16 * STACK_DMAS * round_of(g))
                        store_parts(g, (0, 1))
                    if butterfly == "down mixes":
                        sp.wait_ge(grow, BLOCK_STAGES - 1)
                        sp.dma_start(factors[:], down_factors).then_inc(factors_in, 16)

                def load_ones(r):
                    for t, a, b in ((q_stack[r], 6 * HD, 6 * HD + PARTS), (k_stack[r], 6 * HD + PARTS, SCORE_ROWS_M)):
                        sp.dma_start(t[a:b].rearrange("p h n -> p (h n)"), ones[0:b - a, :]).then_inc(ones_in[r], 16)

                load_x(0, 0)
                for w in range(4):
                    sp.dma_start(wa[:, w], w_attn[:, w]).then_inc(wa_in[w], 16)
                    if w == 0:
                        load_ctx(0)
                sp.dma_start(posi[:], pos).then_inc(pos_in, 16)
                for t, src in ((slope, slopes), (outb, out_bias)):
                    sp.dma_start(t[:], src).then_inc(pos_in, 16)
                sp.dma_start(all_masks.rearrange("p (g b n) -> p g (b n)", g=G, n=P),
                             masks[:, :, 0].rearrange("g p b n -> p g (b n)")).then_inc(all_masks_in, 16)
                for t, src in ((mixw[0], up_mix), (mixw[1], down_mix), (upb, up_bias)):
                    sp.dma_start(t[:], src).then_inc(small_in, 16)
                load_ones(0)
                opening(step)
                sp.wait_ge(masked_ready, 1)
                pipeline(sp, step)
                for r in range(2):
                    for half in range(2):
                        sp.wait_ge(stack_in[r][half], 16 * STACK_DMAS * G // 2)
                for b in range(GB):
                    sp.wait_ge(max_in[b], 16 * G)

            @block.gpsimd
            def _(pool):
                nc.gpsimd.memset(neg_half[:, :], -0.5).then_inc(ident_ready, 1)
                nc.gpsimd.memset(ident[:, :], 0.0).then_inc(ident_ready, 1)
                pool.wait_ge(ident_ready, 2)
                nc.gpsimd.affine_select(out=ident[:, :], in_=ident[:, :], compare_op=ALU.not_equal, fill=1.0,
                                        base=0, pattern=[[-1, P]], channel_multiplier=1).then_inc(ident_ready, 1)
                pool.wait_ge(ident_ready, 3)
                nc.gpsimd.tensor_copy(ident_bf[:, :], ident[:, :]).then_inc(ident_ready, 1)

                def third_parts(g, pieces):
                    for n in pieces:
                        wait_apart(pool, part2_done, 4 * g.n + n + 1)
                        nc.gpsimd.tensor_tensor(parts[:, n, 2], rest[:, n % 2], parts[:, n, 1], ALU.subtract)\
                            .then_inc(parts_done, 1)

                def split_max(g, b):
                    n = 4 * g.n + b + 1
                    nm, t = neg_max[:, b, :], m_tmp[:, b]
                    wait_apart(pool, bank_free[1][1], max_use(g, 2 * b + 1)[1] + 1)
                    nc.gpsimd.tensor_scalar(t[:, 0], nm, 2.0 ** 40, None, ALU.mult).then_inc(m_over, 1)
                    wait_apart(pool, m_over, n)
                    nc.gpsimd.tensor_scalar(t[:, 1], t[:, 0], 0.0, None, ALU.mult).then_inc(m_zero, 1)
                    wait_apart(pool, m_zero, n)
                    nc.gpsimd.tensor_tensor(t[:, 2], nm, t[:, 1], ALU.add).then_inc(m_safe, 1)
                    wait_apart(pool, m_safe, n)
                    nc.gpsimd.tensor_copy(m_parts[:, b, 0], t[:, 2]).then_inc(m_hi, 1)
                    wait_apart(pool, m_hi, n)
                    nc.gpsimd.tensor_tensor(t[:, 3], t[:, 2], m_parts[:, b, 0], ALU.subtract).then_inc(m_rest, 1)
                    wait_apart(pool, m_rest, n)
                    nc.gpsimd.tensor_copy(m_parts[:, b, 1], t[:, 3]).then_inc(m_mid, 1)
                    wait_apart(pool, m_mid, n)
                    nc.gpsimd.tensor_tensor(m_parts[:, b, 2], t[:, 3], m_parts[:, b, 1], ALU.subtract)\
                        .then_inc(m_split, 1)

                def step(butterfly, maxima, attend, project, value):
                    if project and not maxima:
                        norm_rstd(pool, project.n)
                    for b in range(GB):
                        if maxima:
                            split_max(maxima, b)
                        if value and b == 0:
                            third_parts(value, (2,))
                        if project and maxima and b == 0:
                            norm_rstd(pool, project.n)
                        if value and b == 0:
                            third_parts(value, (3,))
                    if butterfly == "products":
                        norm_rstd(pool, G)
                    if project and project.start == 0:
                        for r in range(2):
                            nc.gpsimd.memset(values[r][:], 1.0).then_inc(ones_ready, 1)
                    if project:
                        wait_apart(pool, ctx_high, 2 * project.n + 1)
                        nc.gpsimd.tensor_tensor(cl[:, 0], ctx_raw[:, 0], ch[:, 0].bitcast(F32), ALU.subtract)\
                            .then_inc(ctx_split[0], 1)
                        third_parts(project, (0, 1))

                opening(step)
                pipeline(pool, step)

            @block.scalar
            def _(act):
                def exp(g, i):
                    for q in range(2):
                        act.wait_ge(bank_full[0][q], use(0, "exp", g) + i + 1)
                        if i >= 2 and q == 0:
                            act.wait_ge(pv_full, 8 * g.n + i - 1)
                        nc.scalar.activation(exps[i % 2][:, 4 * q:4 * q + 4, :].rearrange("p h n -> p (h n)"),
                                             SLOT[0][:, q, :], ACT.Exp).then_inc(bank_free[0][q], 1)

                def take_heads(g, b):
                    act.wait_ge(pv_full, 8 * g.n + 2 * b + 2)
                    if b >= 2:
                        act.wait_ge(turn_full, turn_at("heads", g, b - 2) + 1)
                    nc.scalar.activation(heads_t[b % 2][:], PV, ACT.Copy).then_inc(pv_free, 1)

                def take_rows(g, b):
                    act.wait_ge(turn_full, turn_at("rows", g, b) + 1)
                    nc.scalar.activation(max_rows[:, b, :], TURN.bitcast(BF16)[0:PARTS * HEADS, 0:P],
                                         ACT.Copy).then_inc(turn_free, 1)

                def take_values(g, c):
                    bank_is_full(act, 1, "value", g, c)
                    nc.scalar.activation(values[g.start % 2][:, 2 * c:2 * c + 2, :, 0:HD],
                                         SLOT[1][:, c, :].rearrange("p (b h d) -> p b h d", b=2, h=HEADS),
                                         ACT.Copy).then_inc(bank_free[1][c], 1)

                def first_part(g, n):
                    if n % 2 == 0:
                        wait(act, parts_stored[n // 2], 32 * g.n)
                    if n < 2:
                        bank_is_full(act, 0, "query", g, n)
                    else:
                        act.wait_ge(pair_full[n - 2], at(pair_table, "key", g) + 1)
                    src = SLOT[0][:, n, :] if n < 2 else PAIR_BANK[n - 2]
                    nc.scalar.activation(parts[:, n, 0], src, ACT.Copy,
                                         scale=HD ** -0.5 if n < 2 else 1.0).then_inc(part1_done, 1)

                def second_part(g, n):
                    if n < 2:
                        s, count = bank_free[0][n], use(0, "query", g)
                    else:
                        s, count = pair_free[n - 2], at(pair_table, "key", g)
                    act.wait_ge(s, count + 1)
                    nc.scalar.activation(parts[:, n, 1], rest[:, n % 2], ACT.Copy).then_inc(part2_done, 1)

                def take_blocks(n):
                    if n == 0:
                        act.wait_ge(mix_out, N_MIX)
                    act.wait_ge(pre_full, n + 1)
                    nc.scalar.activation(mix_spare[:, 2 * n:2 * n + 2, :], SLOT[0][:, :, 0:DM + 1], ACT.Copy)\
                        .then_inc(pre_free, 1)

                def take_product(n):
                    act.wait_ge(made_full, n + 1)
                    nc.scalar.activation(made_pieces[n][0], SLOT[1].rearrange("p a n -> p (a n)"), ACT.Copy)\
                        .then_inc(made_high, 1)

                for w in range(4):
                    act.wait_ge(wa_in[w], 16)
                    nc.scalar.activation(w_high_part[w][:], wa[:, w], ACT.Copy).then_inc(w_high, 1)

                def step(butterfly, maxima, attend, project, value):
                    if project and project.start == 1:
                        act.wait_ge(all_masks_in, 16)
                        nc.scalar.activation(mask_squares, all_masks, ACT.Square).then_inc(squares_done, 1)
                    for i in range(2 * GB):
                        if attend:
                            exp(attend, i)
                        if attend and i == 0:
                            take_rows(attend, GB - 1)
                        if attend and i >= 2 and i % 2 == 0:
                            take_heads(attend, i // 2 - 1)
                        if value and i < 2:
                            first_part(value, 2 + i)
                        if value and 2 <= i < 4:
                            second_part(value, i)
                        if maxima and i in (4, 6):
                            take_rows(maxima, i // 2 - 2)
                        for n, (src, dst, a, b, o, wfirst, wsecond) in mix_turn(butterfly, i):
                            mix_source_ready(act, n)
                            if n >= MIX_TMP:
                                act.wait_ge(mix_out, n - MIX_TMP + 1)
                            nc.scalar.activation(mix_tmp[:, n % MIX_TMP, 0:src.shape[2]], src[:, a, :], ACT.Copy,
                                                 scale=wfirst).then_inc(mix_first, 1)
                        if butterfly == "products" and i in PRODUCT_TURNS:
                            take_product(PRODUCT_TURNS.index(i))
                    if attend:
                        take_heads(attend, GB - 1)
                    if project:
                        for c in range(2):
                            bank_is_full(act, 0, "turn_x", project, c)
                            nc.scalar.activation(xh[:, c, :], SLOT[0][:, c, :], ACT.Copy).then_inc(x_high, 1)
                    if maxima:
                        take_rows(maxima, 2)
                    if value:
                        if value.start < 2:
                            act.wait_ge(ones_ready, 2)
                        take_values(value, 0)
                    if butterfly == "down mixes":
                        take_blocks(0)
                    if value:
                        take_values(value, 1)
                    if butterfly == "down mixes":
                        take_blocks(1)
                    if attend:
                        for c in range(2):
                            act.wait_ge(pair_full[c], at(pair_table, "attn", attend) + 1)
                            nc.scalar.activation(ah[:, c, :], PAIR_BANK[c], ACT.Copy).then_inc(a_high, 1)
                    if butterfly == "products":
                        take_ffn_tokens(act, 0)
                    if project:
                        act.wait_ge(ctx_in, 16 * (project.n + 1))
                        for c in range(2):
                            nc.scalar.activation(ch[:, c], ctx_raw[:, c], ACT.Copy).then_inc(ctx_high, 1)
                    if butterfly == "down mixes":
                        take_blocks(2)
                        take_blocks(3)
                    if project:
                        first_part(project, 0)
                        first_part(project, 1)
                        second_part(project, 0)
                        second_part(project, 1)

                opening(step)
                pipeline(act, step)

            @block.vector
            def _(dve):
                turned = TURN.rearrange("p (h v) -> p h v", v=VW)

                def reduce_max(g, i):
                    b, s = divmod(i, 2)
                    slot, count = max_use(g, i)
                    for q in range(2):
                        dve.wait_ge(bank_full[slot][q], count + 1)
                        h = s * HH + 4 * q
                        nc.vector.tensor_reduce(neg_max[:, b, h:h + 4], SLOT[slot][:, q, :].rearrange("p (h n) -> p h n", n=P),
                                                AX_X, ALU.max, negate=True).then_inc(bank_free[slot][q], 1)

                def normalise(g, b):
                    n = 4 * g.n + b + 1
                    dve.wait_ge(turn_full, turn_at("heads", g, b) + 1)
                    nc.vector.tensor_scalar(den[:, b % 2], turned[:, :, HD], 1.0, None, ALU.add)\
                        .then_inc(den_done, 1)
                    dve.wait_ge(den_done, n)
                    nc.vector.reciprocal(recip[:, b % 2], den[:, b % 2]).then_inc(recip_done, 1)
                    dve.wait_ge(recip_done, n)
                    nc.vector.tensor_tensor(attn[:, b].rearrange("p (h d) -> p h d", d=HD), turned[:, :, 0:HD],
                                            recip[:, b % 2][:, :, None].to_broadcast([P, HEADS, HD]),
                                            ALU.mult).then_inc(turn_free, 1)

                def make_rest(g, n):
                    dve.wait_ge(part1_done, 4 * g.n + n + 1)
                    wait(dve, parts_done, 4 * g.n + n - 1)
                    src = SLOT[0][:, n, :] if n < 2 else PAIR_BANK[n - 2]
                    nc.vector.scalar_tensor_tensor(rest[:, n % 2], src, HD ** -0.5 if n < 2 else 1.0,
                                                   parts[:, n, 0], ALU.mult, ALU.subtract)\
                        .then_inc((*bank_free[0], *pair_free)[n], 1)

                def grow_blocks(d, k):
                    done = d * (BLOCK_STAGES - 1) + k - 1
                    if k == 1:
                        dve.wait_ge(factors_in, 16 * (d + 1))
                        if d == 1:
                            dve.wait_ge(pre_full, HC // 2)
                        prev = factors[:, 0:FACTOR_AT[1]].rearrange("p (c j) -> p c j", c=HC)
                    else:
                        dve.wait_ge(grow, done)
                        prev = blocks[(k - 1) % 2].rearrange("p c j -> p (c j)")[:, 0:HC * 2 ** k]\
                            .rearrange("p (c j) -> p c j", c=HC)
                    n = 2 ** k
                    fac = factors[:, FACTOR_AT[k]:FACTOR_AT[k] + 2 * HC * n].rearrange("p (c o j) -> p c o j", c=HC, o=2)
                    dst = blocks[k % 2].rearrange("p c j -> p (c j)")[:, 0:2 * HC * n].rearrange(
                        "p (c o j) -> p c o j", c=HC, o=2)
                    nc.vector.tensor_tensor(dst, prev[:, :, None, :].to_broadcast([P, HC, 2, n]), fac, ALU.mult)\
                        .then_inc(grow, 1)

                def split_product_low(n):
                    dve.wait_ge(made_high, n + 1)
                    high, low = made_pieces[n]
                    nc.vector.tensor_tensor(low, SLOT[1].rearrange("p a n -> p (a n)"), high.bitcast(F32), ALU.subtract)\
                        .then_inc(made_free, 1)

                def split_weight(w):
                    dve.wait_ge(w_high, w + 1)
                    nc.vector.tensor_tensor(w_low_part[w][:], wa[:, w], w_high_part[w][:].bitcast(F32), ALU.subtract)\
                        .then_inc(w_split, 1)

                def split_positions():
                    dve.wait_ge(pos_in, 48)
                    for side in range(2):
                        nc.vector.tensor_scalar(posf[:, side], posi[:, side], slope[:, side:side + 1], None,
                                                ALU.mult).then_inc(pos_val, 1)
                    dve.wait_ge(pos_val, 2)
                    nc.vector.tensor_copy(posp[:, :, 0], posf[:]).then_inc(pos_hi, 1)
                    dve.wait_ge(pos_hi, 1)
                    nc.vector.tensor_tensor(posr[:], posf[:], posp[:, :, 0], ALU.subtract).then_inc(pos_rest, 1)
                    dve.wait_ge(pos_rest, 1)
                    nc.vector.tensor_copy(posp[:, :, 1], posr[:]).then_inc(pos_mid, 1)
                    dve.wait_ge(pos_mid, 1)
                    nc.vector.tensor_tensor(bias_sum[:], outb[:, 0], outb[:, 1], ALU.add).then_inc(bias_ready, 1)
                    nc.vector.tensor_tensor(posp[:, :, 2], posr[:], posp[:, :, 1], ALU.subtract).then_inc(pos_split, 1)

                def step(butterfly, maxima, attend, project, value):
                    if project:
                        dve.wait_ge(x_in[project.start % 2], 16 * (round_of(project) + 1))
                    for i in range(2 * GB):
                        if maxima:
                            reduce_max(maxima, i)
                        if project and not maxima and i == 1:
                            norm_apply(dve, project.n, project.n)
                        if value and i in (1, 2):
                            make_rest(value, i + 1)
                        if attend and i >= 3 and i % 2:
                            normalise(attend, (i - 3) // 2)
                        if project and maxima and i < 2:
                            norm_stats(project.n, range(2 * i, 2 * i + 2))
                        if project and i == (2 if maxima else 0):
                            if not maxima:
                                norm_stats(project.n, range(GB))
                            norm_measure(dve, project.n)
                            if project.start == 0:
                                split_weight(0)
                        if project and maxima and i in (4, 5):
                            norm_apply(dve, project.n, project.n, range(2 * i - 8, 2 * i - 6))
                        for n, (src, dst, a, b, o, wfirst, wsecond) in mix_turn(butterfly, i):
                            mix_source_ready(dve, n)
                            dve.wait_ge(mix_first, n + 1)
                            nc.vector.scalar_tensor_tensor(dst[:, o, :], src[:, b, :], wsecond,
                                                           mix_tmp[:, n % MIX_TMP, 0:src.shape[2]], ALU.mult,
                                                           ALU.add).then_inc(mix_out, 1)
                        if butterfly == "down mixes":
                            for k in {6: (1, 2, 3), 7: (4, 5)}.get(i, ()):
                                grow_blocks(0, k)
                        if butterfly == "products" and i == 0:
                            dve.wait_ge(mix_out, 2 * N_MIX)
                            nc.vector.tensor_tensor(hid_bias[:], wet[:, :, DM], upb[:], ALU.add).then_inc(bias_ready, 1)
                        if butterfly == "products" and i - 1 in PRODUCT_TURNS and i != 4:
                            split_product_low(PRODUCT_TURNS.index(i - 1))
                        if butterfly == "products" and i == 2:
                            norm_stats(0, range(GB))
                            norm_measure(dve, G)
                        if butterfly == "products" and i == 6:
                            norm_apply(dve, 0, G)
                    if butterfly == "down mixes":
                        grow_blocks(0, BLOCK_STAGES - 1)
                    if project:
                        if project.start == 0:
                            split_weight(1)
                        for c in range(2):
                            dve.wait_ge(x_high, 2 * project.n + c + 1)
                            nc.vector.tensor_tensor(xl[:, c, :], SLOT[0][:, c, :], xh[:, c, :].bitcast(F32),
                                                    ALU.subtract).then_inc(bank_free[0][c], 1)
                    if attend:
                        normalise(attend, GB - 1)
                        for c in range(2):
                            dve.wait_ge(a_high, 2 * attend.n + c + 1)
                            nc.vector.tensor_tensor(al[:, c, :], PAIR_BANK[c], ah[:, c, :].bitcast(F32),
                                                    ALU.subtract).then_inc(pair_free[c], 1)
                    if butterfly == "products":
                        split_ffn_tokens(dve, 0)
                    if project:
                        dve.wait_ge(ctx_high, 2 * project.n + 2)
                        nc.vector.tensor_tensor(cl[:, 1], ctx_raw[:, 1], ch[:, 1].bitcast(F32), ALU.subtract)\
                            .then_inc(ctx_split[1], 1)
                        if project.start == 0:
                            split_positions()
                        if project.start == 1:
                            dve.wait_ge(squares_done, 1)
                            nc.vector.tensor_reduce(row_least[:], mask_squares, AX_X, ALU.min).then_inc(least_found, 1)
                    if butterfly == "up mixes":
                        for k in range(1, BLOCK_STAGES):
                            grow_blocks(1, k)
                    if value:
                        dve.wait_ge(mask_in, 16 * (value.n + 1))
                        nc.vector.tensor_scalar(mask_add[value.start % 2][:], mask_raw[:], 0.0, MASKED,
                                                ALU.is_equal, ALU.mult).then_inc(mask_ready, 1)
                    if project:
                        for n in range(2):
                            make_rest(project, n)
                        if project.start == 0:
                            split_weight(2)
                            split_weight(3)
                    if attend:
                        for c in range(2):
                            bank_is_full(dve, 1, "output", attend, c)
                            xg = x_all[:, bass.ds(GB * attend.n + 2 * c, 2), :].rearrange("p b n -> p (b n)")
                            nc.vector.tensor_tensor(xg, SLOT[1][:, c, :], xg, ALU.add).then_inc(bank_free[1][c], 1)

                opening(step)
                dve.wait_ge(least_found, 1)
                nc.vector.tensor_scalar(row_masked[:], row_least[:], 0.0, None, ALU.is_equal).then_inc(rows_found, 1)
                dve.wait_ge(masked_full, 1)
                nc.vector.tensor_scalar(masked[:], TURN[:, 0:GB], -2.0, None, ALU.mult).then_inc(masked_ready, 1)
                pipeline(dve, step)

            @block.tensor
            def _(pe):
                pe.wait_ge(ident_ready, 4)

                def score_half(slot, count, r, i, rows, transposed, with_masks):
                    b, s = divmod(i, 2)
                    keep, move = (k_stack[r], q_stack[r]) if transposed else (q_stack[r], k_stack[r])
                    tok = slice(b * P, (b + 1) * P)
                    for q in range(2):
                        wait(pe, bank_free[slot][q], count)
                        dst = SLOT[slot][:, q, :]
                        if with_masks:
                            nc.tensor.matmul(dst.rearrange("p (h n) -> p h n", n=P), ident_bf[:, :],
                                             mask_add[r][:, int(transposed), b:b + 1, :].to_broadcast([P, 4, P]),
                                             start=True, stop=False, skip_group_check=True)
                        for j in range(4):
                            h = s * HH + 4 * q + j
                            last = nc.tensor.matmul(dst[:, j * P:(j + 1) * P], keep[0:rows, h, tok],
                                                    move[0:rows, h, tok], start=(not with_masks and j == 0), stop=(j == 3),
                                                    skip_group_check=True)
                        last.then_inc(bank_full[slot][q], 1)

                def weigh(g, i):
                    b, s = divmod(i, 2)
                    if s == 0 and b:
                        pe.wait_ge(pv_free, 4 * g.n + b)
                    for k in range(HH):
                        if k % 4 == 0:
                            pe.wait_ge(bank_free[0][k // 4], use(0, "exp", g) + i + 1)
                        h = s * HH + k
                        j = k % 4
                        last = nc.tensor.matmul(PV[VW * j:VW * (j + 1), (h // 4) * P:(h // 4 + 1) * P],
                                                values[g.start % 2][:, b, h, :], exps[s][:, k, :], start=True, stop=True)
                    last.then_inc(pv_full, 1)

                def turn_heads(g, b):
                    pe.wait_ge(pv_free, 4 * g.n + b + 1)
                    wait(pe, turn_free, turn_at("heads", g, b))
                    for q in range(4):
                        last = nc.tensor.transpose(TURN[:, q * P:(q + 1) * P],
                                                   heads_t[b % 2][:, q * P:(q + 1) * P], ident[:, :])
                    last.then_inc(turn_full, 1)

                def turn_attn(g, b):
                    pe.wait_ge(turn_free, turn_at("heads", g, b) + 1)
                    for c in range(2):
                        if b == 0:
                            wait(pe, pair_free[c], at(pair_table, "attn", g))
                        last = nc.tensor.transpose(PAIR_BANK[c][:, b * P:(b + 1) * P],
                                                   attn[:, b, c * P:(c + 1) * P], ident[:, :])
                        if b == GB - 1:
                            last.then_inc(pair_full[c], 1)

                def turn_max(g, b):
                    pe.wait_ge(m_split, 4 * g.n + b + 1)
                    wait_apart(pe, turn_free, turn_at("rows", g, b))
                    nc.tensor.transpose(TURN.bitcast(BF16)[0:PARTS * HEADS, 0:P],
                                        m_parts[:, b].rearrange("p a h -> p (a h)"), ident_bf[:, :])\
                        .then_inc(turn_full, 1)

                def turn_others(maxima, attend, i):
                    if maxima and i in (4, 6, 8):
                        turn_max(maxima, i // 2 - 2)
                    if attend and i in (4, 6, 8, 10):
                        turn_attn(attend, i // 2 - 2)

                def split_product(dst, pairs, first_in_bank):
                    terms = [(l, r_) for (lh, ll), (rh, rl) in pairs for l, r_ in ((lh, rh), (ll, rh), (lh, rl))]
                    for i, (l, r_) in enumerate(terms):
                        last = nc.tensor.matmul(dst, l, r_, start=(first_in_bank and i == 0),
                                                stop=(i == len(terms) - 1), skip_group_check=True)
                    return last

                def tokens_product(name, g, c, a_h, a_l, w):
                    wait(pe, bank_free[1][c], use(1, name, g))
                    if c == 0 and g.start == 0:
                        pe.wait_ge(w_split, w + 1)
                    for j in range(2):
                        tok = slice((2 * c + j) * P, (2 * c + j + 1) * P)
                        last = split_product(SLOT[1][:, c, j * DM:(j + 1) * DM],
                                             [((a_h[:, k, tok], a_l[:, k, tok]), (w_high_part[w][:, k, :], w_low_part[w][:, k, :]))
                                              for k in range(KD)], j == 0)
                    last.then_inc(bank_full[1][c], 1)

                def projection(dst, m, w, a_h, a_l):
                    cols = slice(m * P, (m + 1) * P)
                    return split_product(dst, [((w_high_part[w][:, k, cols], w_low_part[w][:, k, cols]), (a_h[:, k, :], a_l[:, k, :]))
                                               for k in range(KD)], True)

                def turn_tokens(g):
                    pe.wait_ge(xn_done, g.n + 1)
                    for c in range(2):
                        wait(pe, bank_free[0][c], use(0, "turn_x", g))
                        for b in range(GB):
                            last = nc.tensor.transpose(SLOT[0][:, c, b * P:(b + 1) * P], xn[:, b, c * P:(c + 1) * P],
                                                       ident[:, :])
                        last.then_inc(bank_full[0][c], 1)

                def exp_blocks(g, n):
                    if n == 0:
                        pe.wait_ge(wet_in, 16)
                        pe.wait_ge(grow, BLOCK_STAGES - 1)
                        pe.wait_ge(bank_free[0][1], use(0, "exp", g) + 2 * GB)
                    else:
                        pe.wait_ge(pre_free, n)
                    for c in range(2):
                        last = nc.tensor.matmul(SLOT[0][:, c, 0:DM + 1], blocks[last_block][:, 2 * n + c, :],
                                                wet[:, 2 * n + c, :], start=True, stop=True)
                    last.then_inc(pre_full, 1)

                def make_product(g, n):
                    if n == 0:
                        pe.wait_ge(bank_free[1][1], use(1, "output", g))
                        pe.wait_ge(mix_out, 2 * N_MIX)
                    elif n == 3:
                        pe.wait_ge(made_high, 3)
                    else:
                        pe.wait_ge(made_free, n - (n > 2))
                        if n == 2:
                            pe.wait_ge(grow, 2 * (BLOCK_STAGES - 1))
                    for q in range(2):
                        for j in range(4 if n < 3 else 2):
                            if n < 2:
                                last = nc.tensor.transpose(SLOT[1][:, q, j * P:(j + 1) * P],
                                                           wet[:, 4 * q + j, n * P:(n + 1) * P], ident[:, :])
                            elif n == 2:
                                last = nc.tensor.transpose(SLOT[1][:, q, j * P:(j + 1) * P],
                                                           blocks[last_block][:, 4 * q + j, :], ident[:, :])
                            else:
                                c = 4 * (n - 3) + 2 * q + j
                                last = nc.tensor.matmul(SLOT[1][:, q, j * DM:(j + 1) * DM], blocks[1 - last_block][:, c, :],
                                                        down_a[:, c, :], start=(j == 0), stop=True, skip_group_check=True)
                    last.then_inc(made_full, 1)

                def step(with_masks, butterfly, maxima, attend, project, value):
                    if butterfly == "up mixes":
                        pe.wait_ge(pre_free, HC // 2)
                    if maxima and maxima.start == 0:
                        pe.wait_ge(ones_in[0], 32)
                    if maxima and maxima.start == 1:
                        pe.wait_ge(ones_in[1], 32)
                    if maxima:
                        pe.wait_ge(mask_ready, maxima.n + 1)
                    for i in range(2 * GB + 3):
                        b, s = divmod(i, 2)
                        if attend and i < 2 * GB:
                            if s == 0:
                                pe.wait_ge(max_in[b], 16 * (attend.n + 1))
                            score_half(0, use(0, "exp", attend) + i, attend.start % 2, i, SCORE_ROWS_M, True, with_masks)
                        if maxima and i < 2 * GB:
                            if i % GB == 0:
                                pe.wait_ge(stack_in[maxima.start % 2][i // GB], 16 * STACK_DMAS * (round_of(maxima) + 1))
                            score_half(*max_use(maxima, i), maxima.start % 2, i, SCORE_ROWS, False, with_masks)
                        if value and i < 2:
                            if i == 0:
                                for c in range(2):
                                    pe.wait_ge(ctx_split[c], value.n + 1)
                                if value.start == 0:
                                    pe.wait_ge(w_split, 2)
                            wait(pe, pair_free[i], at(pair_table, "key", value))
                            projection(PAIR_BANK[i], i, 1, ch, cl).then_inc(pair_full[i], 1)
                        if attend and s == 1 and b >= 1:
                            turn_heads(attend, b - 1)
                        if attend and i == 0:
                            turn_max(attend, GB - 1)
                        if i < 2 * GB:
                            turn_others(maxima, attend, i)
                        if butterfly == "products" and i == 2 * GB + 1:
                            pe.wait_ge(bank_free[0][1], use(0, "exp", attend) + 2 * GB)
                            turn_ffn_tokens(pe, 0)
                        if attend and 1 <= i <= 2 * GB:
                            weigh(attend, i - 1)
                        if project and maxima and i == 2 * GB:
                            turn_tokens(project)
                        if i >= 2 * GB:
                            turn_others(maxima, attend, i)
                        if butterfly == "products" and i in PRODUCT_TURNS:
                            make_product(attend, PRODUCT_TURNS.index(i))
                        if butterfly == "down mixes" and i > 2 * GB:
                            exp_blocks(attend, i - 2 * GB - 1)
                        if value and i == 2 * GB:
                            tokens_product("value", value, 0, ch, cl, 2)
                        if value and i == 2 * GB + 1:
                            tokens_product("value", value, 1, ch, cl, 2)
                        if project and not maxima and i == 2 * GB + 1:
                            turn_tokens(project)
                    if project:
                        for c in range(2):
                            pe.wait_ge(bank_free[0][c], use(0, "query", project))
                        if project.start == 0:
                            pe.wait_ge(w_split, 1)
                        for m in range(2):
                            projection(SLOT[0][:, m, :], m, 0, xh, xl).then_inc(bank_full[0][m], 1)
                    if butterfly == "down mixes":
                        exp_blocks(attend, 2)
                    if attend:
                        if butterfly == "products":
                            pe.wait_ge(made_free, 4)
                        for c in range(2):
                            pe.wait_ge(pair_free[c], at(pair_table, "attn", attend) + 1)
                        for c in range(2):
                            tokens_product("output", attend, c, ah, al, 3)
                    if butterfly == "down mixes":
                        exp_blocks(attend, 3)

                opening(partial(step, True))
                pe.wait_ge(rows_found, 1)
                nc.tensor.matmul(TURN[:, 0:GB], row_masked[:, 0:1].to_broadcast([P, P]), neg_half[:, :],
                                 start=True, stop=True).then_inc(masked_full, 1)
                step(True, None, *groups(0))
                pe.wait_ge(masked_ready, 1)
                any_masked = pe.value_load(masked[0:1, 0:1], min_val=0, max_val=P)
                with pe.If(any_masked > 0):
                    pipeline(pe, partial(step, True), 1)
                with pe.Else():
                    pipeline(pe, partial(step, False), 1)

        HB = [psum[:, i, :] for i in (2, 3, 6, 7)]
        Y = [psum[:, 4 + c, :] for c in range(2)]

        with nc.Block() as block:
            @block.sync
            def _(sp):
                with sp.Fori(0, G) as g:
                    wait_apart(sp, y_done, 2 * g + 2)
                    sp.dma_start(out[bass.ds(GB * g, GB)].rearrange("b p n -> p b n"), y_out[:]).then_inc(stored, 16)
                sp.wait_ge(stored, 16 * G)

            @block.gpsimd
            def _(pool):
                def residual(g):
                    wait_apart(pool, stored, 16 * g)
                    nc.gpsimd.tensor_tensor(x_res[:], x_all[:, bass.ds(GB * g, GB), :],
                                            bias_sum[:, None, :].to_broadcast([P, GB, DM]), ALU.add)\
                        .then_inc(res_ready, 1)

                residual(0)
                with pool.Fori(1, G) as g:
                    norm_rstd(pool, g + G)
                    residual(g)

            @block.scalar
            def _(act):
                def hidden(g):
                    for c in range(HC):
                        act.wait_ge(h_full, 8 * g + c + 1)
                        buf = c % HID_BUFS
                        if c >= HID_BUFS:
                            act.wait_ge(ffn_used, 8 * g + c - HID_BUFS + 1)
                        nc.scalar.activation(gf[:, buf], HB[buf], ACT.Gelu, bias=hid_bias[:, c:c + 1])
                        nc.scalar.activation(gh[:, buf], HB[buf], ACT.Gelu, bias=hid_bias[:, c:c + 1])\
                            .then_inc(g_done, 1)

                with act.Fori(0, G - 1) as g:
                    hidden(g)
                    take_ffn_tokens(act, g + 1)
                hidden(G - 1)

            @block.vector
            def _(dve):
                def hidden(g, chunks):
                    for c in chunks:
                        dve.wait_ge(g_done, 8 * g + c + 1)
                        buf = c % HID_BUFS
                        nc.vector.tensor_tensor(gl[:, buf], gf[:, buf], gh[:, buf].bitcast(F32), ALU.subtract)\
                            .then_inc(g_split, 1)

                def finish(g):
                    dve.wait_ge(res_ready, g + 1)
                    dve.wait_ge(ffn_used, 8 * g + 8)
                    for c in range(2):
                        nc.vector.tensor_tensor(y_out[:, 2 * c:2 * c + 2].rearrange("p b n -> p (b n)"), Y[c],
                                                x_res[:, 2 * c:2 * c + 2].rearrange("p b n -> p (b n)"), ALU.add)\
                            .then_inc(y_done, 1)

                with dve.Fori(0, G - 1) as g:
                    hidden(g, range(2))
                    norm_stats(g + 1, range(GB))
                    norm_measure(dve, g + 1 + G)
                    hidden(g, range(2, 5))
                    norm_apply(dve, g + 1, g + 1 + G)
                    hidden(g, range(5, HC))
                    split_ffn_tokens(dve, g + 1)
                    finish(g)
                hidden(G - 1, range(HC))
                finish(G - 1)

            @block.tensor
            def _(pe):
                def up(g, c):
                    if c >= HID_BUFS:
                        pe.wait_ge(g_done, 8 * g + c - HID_BUFS + 1)
                    n = 0
                    cols = slice(c * P, (c + 1) * P)
                    for k in range(KD):
                        for w, t in ((w1h, xh), (w1l, xh), (w1h, xl)):
                            last = nc.tensor.matmul(HB[c % HID_BUFS], w[:, k, cols], t[:, k, :], start=(n == 0),
                                                    stop=(n == 5))
                            n += 1
                    last.then_inc(h_full, 1)

                def down(g, c):
                    pe.wait_ge(g_split, 8 * g + c + 1)
                    for b in range(GB):
                        tok = slice(b * P, (b + 1) * P)
                        for i, (t, w) in enumerate(((gh, w2h), (gl, w2h), (gh, w2l))):
                            last = nc.tensor.matmul(Y[b // 2][:, (b % 2) * DM:(b % 2 + 1) * DM], t[:, c % HID_BUFS, tok],
                                                    w[:, c, :], start=(c == 0 and i == 0 and b % 2 == 0),
                                                    stop=(c == HC - 1 and i == 2), skip_group_check=True)
                    last.then_inc(ffn_used, 1)

                def group_ffn(g, ahead):
                    for c in range(2):
                        pe.wait_ge(t_free[c], g + 1)
                    for c in range(HC):
                        up(g, c)
                        if c >= LAG and c < HC - 1:
                            down(g, c - LAG)
                    if ahead:
                        turn_ffn_tokens(pe, g + 1)
                    for c in range(HC - 1 - LAG, HC):
                        down(g, c)

                with pe.Fori(0, G - 1) as g:
                    group_ffn(g, True)
                group_ffn(G - 1, False)


def _mix_weights(w, np):
    out = np.empty((P, MIX_STAGES, HC // 2, 4), w.dtype)
    for k, _, _, pair in MIX_UP:
        out[:, k, pair] = w[BLOCK_STAGES + k, pair * P:(pair + 1) * P].reshape(P, 4)
    return out


def _block_factors(w, np):
    i = np.arange(P)[:, None, None, None]
    c = np.arange(HC)[None, :, None, None]
    out = []
    for k in range(BLOCK_STAGES):
        o = np.arange(2)[None, None, :, None]
        low = np.arange(2 ** k)[None, None, None, :]
        pair = (c * P + i >> (k + 1)) * 2 ** k + low
        out.append(w[k][pair, o, (i >> k) & 1].reshape(P, -1))
    return np.concatenate(out, 1)


def kernel(x, ctx_1024, itok_BxS_8_8191, itok_BxS2_1_8191, mask_BxSxS2_if1, L0_xattn_W_q, L0_xattn_W_k,
           L0_xattn_W_v, L0_xattn_W_o, L0_ffn_W_exp, L0_ffn_b_exp, L0_ffn_up_weights, L0_ffn_up_bias,
           L0_ffn_down_weights, L0_ffn_W_con, L0_ffn_b_con, L0_ffn_down_bias):
    import numpy as np
    import concourse.bacc as bacc
    from concourse.bass_utils import run_bass_kernel_spmd

    def arr(a):
        return np.asarray(a)

    mask = arr(mask_BxSxS2_if1).reshape(G, GB, P, P)
    pos = np.stack([arr(itok_BxS_8_8191), arr(itok_BxS2_1_8191)], 0).reshape(2, G, 1, GT)
    ratio = 2.0 ** (-8.0 / HEADS)
    slope = np.array([ratio ** i for i in range(1, HEADS + 1)], np.float32)

    def by_chunk(a):
        return a.reshape(-1, P, a.shape[-1]).transpose(1, 0, 2)

    def side_order(w):
        return w.T.reshape(DM, HEADS, HD).transpose(0, 2, 1).reshape(DM, DM)

    weights = [side_order(arr(L0_xattn_W_q)), side_order(arr(L0_xattn_W_k)), arr(L0_xattn_W_v).T, arr(L0_xattn_W_o).T]
    arrays = {
        "x": arr(x),
        "ctx_t": arr(ctx_1024).reshape(G, GT, KD, P).transpose(0, 3, 2, 1),
        "masks": np.stack([mask.transpose(0, 2, 1, 3), mask.transpose(0, 3, 1, 2)], 2),
        "pos": np.broadcast_to(pos, (2, G, HEADS, GT)).reshape(2, P, GT).transpose(1, 0, 2),
        "slopes": np.tile(np.stack([-slope, slope], 1), (G, 1)),
        "w_attn": np.stack([by_chunk(w) for w in weights], 1),
        "w_exp_t": by_chunk(np.concatenate([arr(L0_ffn_W_exp).T, arr(L0_ffn_b_exp)[:, None]], 1)),
        "w_con": by_chunk(arr(L0_ffn_W_con)),
        "up_bias": arr(L0_ffn_up_bias).reshape(HC, P).T,
        "out_bias": np.broadcast_to(np.stack([arr(L0_ffn_b_con), arr(L0_ffn_down_bias)]), (P, 2, DM)),
        "up_factors": _block_factors(arr(L0_ffn_up_weights), np),
        "down_factors": _block_factors(arr(L0_ffn_down_weights), np),
        "up_mix": _mix_weights(arr(L0_ffn_up_weights), np),
        "down_mix": _mix_weights(arr(L0_ffn_down_weights), np),
        "ones": np.ones((2 * PARTS, HEADS * GT), mybir.dt.np(BF16)),
    }
    arrays = {n: np.ascontiguousarray(a) for n, a in arrays.items()}
    nc = bacc.Bacc("TRN2", target_bir_lowering=False, num_devices=1)
    args = [nc.dram_tensor(f"in_{n}", a.shape, mybir.dt.from_np(a.dtype), kind="ExternalInput").ap()
            for n, a in arrays.items()]
    args.append(nc.dram_tensor("out_x", (BATCHES, P, DM), F32, kind="ExternalOutput").ap())
    build(nc, *args)
    r = run_bass_kernel_spmd(nc, [{f"in_{n}": a for n, a in arrays.items()}], core_ids=[0])
    return r.results[0]["out_x"]
```
